# Optimizing a Trainium2 kernel written in Bass

```python
import numpy as np
import jax
import jax.numpy as jnp

def _softmax(x, axis=-1):
    return jax.nn.softmax(x, axis=axis)

def _gelu(x):
    return jax.nn.gelu(x, approximate=True)

def _silu(x):
    return jax.nn.silu(x)

def _sigmoid(x):
    return jax.nn.sigmoid(x)

def _layernorm(x, axis=-1, eps=1e-05):
    m = jnp.mean(x, axis=axis, keepdims=True)
    v = jnp.var(x, axis=axis, keepdims=True)
    return (x - m) / jnp.sqrt(v + eps)

def _scatter_add(tgt, idx, src, axis=0):
    return tgt.at[idx].add(src)

def _segment_sum(src, seg, n):
    return jax.ops.segment_sum(src, seg, n)
kernel_name = 'mk_dlrm_tower_d1_rec_r8_14ba2b'

def setup_inputs(seed: int=0):
    np.random.seed(seed)
    _w = jnp.asarray

    def _rec_inputs():
        import jax
        import jax.numpy as jnp
        _tk = jax.random.key(seed)
        dense_ctx = jax.random.normal(jax.random.fold_in(_tk, 190), (512, 16), jnp.float32)
        ids = jnp.stack([jax.random.randint(jax.random.fold_in(_tk, 200 + f), (512,), 0, v, jnp.int32) for f, v in enumerate([1000, 1250, 125000, 12500, 12500, 12500, 12500, 1000, 125000, 12500, 12500, 12500, 12500, 125000, 1250, 1000, 125000, 12500, 1000, 125000, 12500, 1000, 1250, 125000, 1000, 125000, 1250, 1250, 12500, 1250, 1250, 125000])], axis=1)
        tbl_0 = 0.05 * jax.random.normal(jax.random.fold_in(_tk, 500 + 0), (1000, 16), jnp.float32)
        tbl_1 = 0.05 * jax.random.normal(jax.random.fold_in(_tk, 500 + 1), (1250, 16), jnp.float32)
        tbl_2 = 0.05 * jax.random.normal(jax.random.fold_in(_tk, 500 + 2), (125000, 16), jnp.float32)
        tbl_3 = 0.05 * jax.random.normal(jax.random.fold_in(_tk, 500 + 3), (12500, 16), jnp.float32)
        tbl_4 = 0.05 * jax.random.normal(jax.random.fold_in(_tk, 500 + 4), (12500, 16), jnp.float32)
        tbl_5 = 0.05 * jax.random.normal(jax.random.fold_in(_tk, 500 + 5), (12500, 16), jnp.float32)
        tbl_6 = 0.05 * jax.random.normal(jax.random.fold_in(_tk, 500 + 6), (12500, 16), jnp.float32)
        tbl_7 = 0.05 * jax.random.normal(jax.random.fold_in(_tk, 500 + 7), (1000, 16), jnp.float32)
        tbl_8 = 0.05 * jax.random.normal(jax.random.fold_in(_tk, 500 + 8), (125000, 16), jnp.float32)
        tbl_9 = 0.05 * jax.random.normal(jax.random.fold_in(_tk, 500 + 9), (12500, 16), jnp.float32)
        tbl_10 = 0.05 * jax.random.normal(jax.random.fold_in(_tk, 500 + 10), (12500, 16), jnp.float32)
        tbl_11 = 0.05 * jax.random.normal(jax.random.fold_in(_tk, 500 + 11), (12500, 16), jnp.float32)
        tbl_12 = 0.05 * jax.random.normal(jax.random.fold_in(_tk, 500 + 12), (12500, 16), jnp.float32)
        tbl_13 = 0.05 * jax.random.normal(jax.random.fold_in(_tk, 500 + 13), (125000, 16), jnp.float32)
        tbl_14 = 0.05 * jax.random.normal(jax.random.fold_in(_tk, 500 + 14), (1250, 16), jnp.float32)
        tbl_15 = 0.05 * jax.random.normal(jax.random.fold_in(_tk, 500 + 15), (1000, 16), jnp.float32)
        tbl_16 = 0.05 * jax.random.normal(jax.random.fold_in(_tk, 500 + 16), (125000, 16), jnp.float32)
        tbl_17 = 0.05 * jax.random.normal(jax.random.fold_in(_tk, 500 + 17), (12500, 16), jnp.float32)
        tbl_18 = 0.05 * jax.random.normal(jax.random.fold_in(_tk, 500 + 18), (1000, 16), jnp.float32)
        tbl_19 = 0.05 * jax.random.normal(jax.random.fold_in(_tk, 500 + 19), (125000, 16), jnp.float32)
        tbl_20 = 0.05 * jax.random.normal(jax.random.fold_in(_tk, 500 + 20), (12500, 16), jnp.float32)
        tbl_21 = 0.05 * jax.random.normal(jax.random.fold_in(_tk, 500 + 21), (1000, 16), jnp.float32)
        tbl_22 = 0.05 * jax.random.normal(jax.random.fold_in(_tk, 500 + 22), (1250, 16), jnp.float32)
        tbl_23 = 0.05 * jax.random.normal(jax.random.fold_in(_tk, 500 + 23), (125000, 16), jnp.float32)
        tbl_24 = 0.05 * jax.random.normal(jax.random.fold_in(_tk, 500 + 24), (1000, 16), jnp.float32)
        tbl_25 = 0.05 * jax.random.normal(jax.random.fold_in(_tk, 500 + 25), (125000, 16), jnp.float32)
        tbl_26 = 0.05 * jax.random.normal(jax.random.fold_in(_tk, 500 + 26), (1250, 16), jnp.float32)
        tbl_27 = 0.05 * jax.random.normal(jax.random.fold_in(_tk, 500 + 27), (1250, 16), jnp.float32)
        tbl_28 = 0.05 * jax.random.normal(jax.random.fold_in(_tk, 500 + 28), (12500, 16), jnp.float32)
        tbl_29 = 0.05 * jax.random.normal(jax.random.fold_in(_tk, 500 + 29), (1250, 16), jnp.float32)
        tbl_30 = 0.05 * jax.random.normal(jax.random.fold_in(_tk, 500 + 30), (1250, 16), jnp.float32)
        tbl_31 = 0.05 * jax.random.normal(jax.random.fold_in(_tk, 500 + 31), (125000, 16), jnp.float32)
        _rk = jax.random.fold_in(_tk, 7)
        W_top1 = 0.0606339 * jax.random.normal(jax.random.fold_in(_tk, 801), (272, 512), jnp.float32)
        W_top2 = 0.0441942 * jax.random.normal(jax.random.fold_in(_tk, 802), (512, 256), jnp.float32)
        W_top3 = 0.0625 * jax.random.normal(jax.random.fold_in(_tk, 803), (256, 1), jnp.float32)
        b_top1 = jnp.zeros((512,), jnp.float32)
        b_top2 = jnp.zeros((256,), jnp.float32)
        return (dense_ctx, ids, tbl_0, tbl_1, tbl_2, tbl_3, tbl_4, tbl_5, tbl_6, tbl_7, tbl_8, tbl_9, tbl_10, tbl_11, tbl_12, tbl_13, tbl_14, tbl_15, tbl_16, tbl_17, tbl_18, tbl_19, tbl_20, tbl_21, tbl_22, tbl_23, tbl_24, tbl_25, tbl_26, tbl_27, tbl_28, tbl_29, tbl_30, tbl_31, W_top1, b_top1, W_top2, b_top2, W_top3)
    dense_ctx, ids, tbl_0, tbl_1, tbl_2, tbl_3, tbl_4, tbl_5, tbl_6, tbl_7, tbl_8, tbl_9, tbl_10, tbl_11, tbl_12, tbl_13, tbl_14, tbl_15, tbl_16, tbl_17, tbl_18, tbl_19, tbl_20, tbl_21, tbl_22, tbl_23, tbl_24, tbl_25, tbl_26, tbl_27, tbl_28, tbl_29, tbl_30, tbl_31, W_top1, b_top1, W_top2, b_top2, W_top3 = _rec_inputs()

    def _L0_rec_setup():
        import jax, jax.numpy as jnp
        import numpy as np
        NUM_FIELDS = 32
        EMBED_DIM = 16
        BATCH = 512
        CROSS_SIZES = [128, 128, 128]

        def _cin_forward(x, Ws, bs):
            x0 = x
            h = x
            xs = []
            n_layers = len(Ws)
            for i in range(n_layers):
                B, F, E = x0.shape
                G = h.shape[1]
                z = (x0[:, :, None, :] * h[:, None, :, :]).reshape(B, F * G, E)
                y = jax.nn.relu(jnp.einsum('oc,bce->boe', Ws[i], z) + bs[i][None, :, None])
                if i != n_layers - 1:
                    half = y.shape[1] // 2
                    x_keep, h = (y[:, :half, :], y[:, half:, :])
                else:
                    x_keep, h = (y, y)
                xs.append(x_keep)
            return jnp.sum(jnp.concatenate(xs, axis=1), axis=2)
        key = jax.random.key(seed)
        ks = jax.random.split(key, 8)
        x = jax.random.normal(ks[0], (BATCH, NUM_FIELDS, EMBED_DIM), dtype=jnp.float32)
        prev = NUM_FIELDS
        inp = {'x': x}
        for i, cs in enumerate(CROSS_SIZES):
            in_ch = NUM_FIELDS * prev
            scale = 1.0 / np.sqrt(in_ch)
            inp[f'W{i}'] = jax.random.uniform(ks[1 + 2 * i], (cs, in_ch), dtype=jnp.float32, minval=-scale, maxval=scale)
            inp[f'b{i}'] = jax.random.uniform(ks[2 + 2 * i], (cs,), dtype=jnp.float32, minval=-scale, maxval=scale)
            prev = cs // 2
        return inp
    _L0_rec_all = _L0_rec_setup()
    _L0_rec_in = {k: v for k, v in _L0_rec_all.items() if k in ('W0', 'b0', 'W1', 'b1', 'W2', 'b2')}
    del _L0_rec_all
    return {'dense_ctx': dense_ctx, 'ids': ids, 'tbl_0': tbl_0, 'tbl_1': tbl_1, 'tbl_2': tbl_2, 'tbl_3': tbl_3, 'tbl_4': tbl_4, 'tbl_5': tbl_5, 'tbl_6': tbl_6, 'tbl_7': tbl_7, 'tbl_8': tbl_8, 'tbl_9': tbl_9, 'tbl_10': tbl_10, 'tbl_11': tbl_11, 'tbl_12': tbl_12, 'tbl_13': tbl_13, 'tbl_14': tbl_14, 'tbl_15': tbl_15, 'tbl_16': tbl_16, 'tbl_17': tbl_17, 'tbl_18': tbl_18, 'tbl_19': tbl_19, 'tbl_20': tbl_20, 'tbl_21': tbl_21, 'tbl_22': tbl_22, 'tbl_23': tbl_23, 'tbl_24': tbl_24, 'tbl_25': tbl_25, 'tbl_26': tbl_26, 'tbl_27': tbl_27, 'tbl_28': tbl_28, 'tbl_29': tbl_29, 'tbl_30': tbl_30, 'tbl_31': tbl_31, 'W_top1': W_top1, 'b_top1': b_top1, 'W_top2': W_top2, 'b_top2': b_top2, 'W_top3': W_top3, 'L0_rec_W0': _L0_rec_in['W0'], 'L0_rec_b0': _L0_rec_in['b0'], 'L0_rec_W1': _L0_rec_in['W1'], 'L0_rec_b1': _L0_rec_in['b1'], 'L0_rec_W2': _L0_rec_in['W2'], 'L0_rec_b2': _L0_rec_in['b2']}

def reference(dense_ctx, ids, tbl_0, tbl_1, tbl_2, tbl_3, tbl_4, tbl_5, tbl_6, tbl_7, tbl_8, tbl_9, tbl_10, tbl_11, tbl_12, tbl_13, tbl_14, tbl_15, tbl_16, tbl_17, tbl_18, tbl_19, tbl_20, tbl_21, tbl_22, tbl_23, tbl_24, tbl_25, tbl_26, tbl_27, tbl_28, tbl_29, tbl_30, tbl_31, W_top1, b_top1, W_top2, b_top2, W_top3, L0_rec_W0, L0_rec_b0, L0_rec_W1, L0_rec_b1, L0_rec_W2, L0_rec_b2):
    import jax
    import jax.numpy as jnp

    def _L0_rec_ref(x, W0, b0, W1, b1, W2, b2):
        import jax, jax.numpy as jnp
        import numpy as np
        NUM_FIELDS = 32
        EMBED_DIM = 16
        BATCH = 512
        CROSS_SIZES = [128, 128, 128]

        def _cin_forward(x, Ws, bs):
            x0 = x
            h = x
            xs = []
            n_layers = len(Ws)
            for i in range(n_layers):
                B, F, E = x0.shape
                G = h.shape[1]
                z = (x0[:, :, None, :] * h[:, None, :, :]).reshape(B, F * G, E)
                y = jax.nn.relu(jnp.einsum('oc,bce->boe', Ws[i], z) + bs[i][None, :, None])
                if i != n_layers - 1:
                    half = y.shape[1] // 2
                    x_keep, h = (y[:, :half, :], y[:, half:, :])
                else:
                    x_keep, h = (y, y)
                xs.append(x_keep)
            return jnp.sum(jnp.concatenate(xs, axis=1), axis=2)
        return _cin_forward(x, [W0, W1, W2], [b0, b1, b2])
    e = jnp.stack([tbl_0[ids[:, 0]], tbl_1[ids[:, 1]], tbl_2[ids[:, 2]], tbl_3[ids[:, 3]], tbl_4[ids[:, 4]], tbl_5[ids[:, 5]], tbl_6[ids[:, 6]], tbl_7[ids[:, 7]], tbl_8[ids[:, 8]], tbl_9[ids[:, 9]], tbl_10[ids[:, 10]], tbl_11[ids[:, 11]], tbl_12[ids[:, 12]], tbl_13[ids[:, 13]], tbl_14[ids[:, 14]], tbl_15[ids[:, 15]], tbl_16[ids[:, 16]], tbl_17[ids[:, 17]], tbl_18[ids[:, 18]], tbl_19[ids[:, 19]], tbl_20[ids[:, 20]], tbl_21[ids[:, 21]], tbl_22[ids[:, 22]], tbl_23[ids[:, 23]], tbl_24[ids[:, 24]], tbl_25[ids[:, 25]], tbl_26[ids[:, 26]], tbl_27[ids[:, 27]], tbl_28[ids[:, 28]], tbl_29[ids[:, 29]], tbl_30[ids[:, 30]], tbl_31[ids[:, 31]]], axis=1)
    z = _L0_rec_ref(e, L0_rec_W0, L0_rec_b0, L0_rec_W1, L0_rec_b1, L0_rec_W2, L0_rec_b2)
    z = z.reshape(z.shape[0], -1)
    h = jnp.concatenate([z, dense_ctx], axis=1)
    h = jnp.maximum(h @ W_top1 + b_top1, 0.0)
    h = jnp.maximum(h @ W_top2 + b_top2, 0.0)
    y = h @ W_top3
    return y

_drawn_inputs = setup_inputs


def setup_inputs(seed=0):
    import zlib

    import numpy as np

    out = dict(_drawn_inputs(seed))
    spreads = {'b_top1': (0.0, 0.362), 'b_top2': (0.0, 0.401)}
    factors = {'tbl_0': 8.0,
     'tbl_1': 8.0,
     'tbl_2': 8.0,
     'tbl_3': 8.0,
     'tbl_4': 8.0,
     'tbl_5': 8.0,
     'tbl_6': 8.0,
     'tbl_7': 8.0,
     'tbl_8': 8.0,
     'tbl_9': 8.0,
     'tbl_10': 8.0,
     'tbl_11': 8.0,
     'tbl_12': 8.0,
     'tbl_13': 8.0,
     'tbl_14': 8.0,
     'tbl_15': 8.0,
     'tbl_16': 8.0,
     'tbl_17': 8.0,
     'tbl_18': 8.0,
     'tbl_19': 8.0,
     'tbl_20': 8.0,
     'tbl_21': 8.0,
     'tbl_22': 8.0,
     'tbl_23': 8.0,
     'tbl_24': 8.0,
     'tbl_25': 8.0,
     'tbl_26': 8.0,
     'tbl_27': 8.0,
     'tbl_28': 8.0,
     'tbl_29': 8.0,
     'tbl_30': 8.0,
     'tbl_31': 8.0,
     'L0_rec_W0': 8.0,
     'L0_rec_W1': 8.0,
     'L0_rec_W2': 8.0,
     'L0_rec_b0': 4.651,
     'L0_rec_b1': 6.843,
     'L0_rec_b2': 7.272}
    for name, (base, spread) in spreads.items():
        noise = np.random.default_rng([zlib.crc32(name.encode()), seed]).standard_normal(out[name].shape)
        drawn = base * np.exp(spread * noise) if base else spread * noise
        out[name] = jnp.asarray(drawn.astype(out[name].dtype))
    for name, factor in factors.items():
        out[name] = (out[name] * factor).astype(out[name].dtype)
    return out
```

```python
from contextlib import ExitStack

import concourse.bass as bass
from concourse import mybir

F32 = mybir.dt.float32
F32R = mybir.dt.float32r
I32 = mybir.dt.int32
U32 = mybir.dt.uint32
ALU = mybir.AluOpType
ACT = mybir.ActivationFunctionType
AX_X = mybir.AxisListType.X

P = 128
FIELDS, E, BATCH, DENSE = 32, 16, 512, 16
HALF = 64
HID1, HID2 = 512, 256
BT = BATCH // P
EQ = 4
TPB = E // EQ
CT = BT * TPB
N = EQ * P
GC = 4
ZSLOTS, SSLOTS = 3, 2
REST = FIELDS // 2

WHOLE, SPLIT = "whole", "split"
KIND = {(0, 0): WHOLE,
        (1, 0): SPLIT, (1, 1): SPLIT, (1, 2): SPLIT, (1, 3): WHOLE,
        (2, 0): SPLIT, (2, 1): SPLIT, (2, 2): SPLIT, (2, 3): WHOLE}
SPLITS = [k for k in KIND if KIND[k] == SPLIT]
WHOLES = [k for k in KIND if KIND[k] == WHOLE]

L0, L1, L2 = [(0, 0)], [(1, g) for g in range(4)], [(2, g) for g in range(4)]

PLAN = {q: L1 + L2 + L0 if q == 4 else L1 + L0 + L2 for q in range(1, 5)}
SPLIT_OF = {q: [k for k in PLAN[q] if KIND[k] == SPLIT] for q in PLAN}
BY_POOL = {q: [k for k in SPLIT_OF[q] if q != 1] for q in PLAN}
BY_DVE = {q: [k for k in SPLIT_OF[q] if k not in BY_POOL[q]] for q in PLAN}
PER = len(PLAN[1])
assert PER % ZSLOTS == 0 and len(SPLITS) % SSLOTS == 0 and KIND[0, 0] == WHOLE


def tile(i, q, layer):
    n = q + (1, 0, -1)[layer]
    return i + n // TPB, n % TPB


def opening(i):
    return isinstance(i, int) and i < 0


def exists(i, q, key):
    return not isinstance(i, int) or 0 <= TPB * i + q + (1, 0, -1)[key[0]] < CT


def walk(members, i, q, key, step):
    n = members[q].index(key) + step
    while n < 0:
        i, q = (i - 1, 4) if q == 1 else (i, q - 1)
        n += len(members[q])
    while n >= len(members[q]):
        n -= len(members[q])
        i, q = (i + 1, 1) if q == 4 else (i, q + 1)
    return i, q, members[q][n]


def place(members, i, q, key):
    return (i + 1) * sum(map(len, members.values())) + sum(len(members[k]) for k in range(1, q)) + members[q].index(key)


def first(members):
    return min(place(members, i, q, k) for i in (-1, 0) for q in members for k in members[q] if exists(i, q, k))


def count(members, i, q, key):
    return place(members, i, q, key) - first(members) + 1


def amount(members, i, q, key):
    n = 1
    while isinstance(i, int) and not exists(*(at := walk(members, i, q, key, n))) and at[0] < BT:
        n += 1
    return n


def user_before(members, ring, i, q, key):
    at = walk(members, i, q, key, -ring)
    while not exists(*at):
        if isinstance(at[0], int) and at[0] < -1:
            return None
        at = walk(members, *at, -ring)
    return at


def zslot(q, key):
    return PLAN[q].index(key) % ZSLOTS


def sslot(q, key):
    return place(SPLIT_OF, 0, q, key) % SSLOTS


def peeled_rounds(engine, round_):
    for q in (3, 4):
        round_(-1, q)
    with engine.Fori(0, BT - 1) as i:
        for q in range(1, 5):
            round_(i, q)
    for q in range(1, 5):
        round_(BT - 1, q)


def cin_tower(nc, t, out):
    with ExitStack() as ctx:
        def sb(name, shape, dt=F32):
            return ctx.enter_context(nc.sbuf_tensor(name, shape, dt))

        def bank(name, dt=F32):
            return ctx.enter_context(nc.psum_tensor(name, [P, N], dt))

        def sem(name):
            return ctx.enter_context(nc.semaphore(name))

        xx = nc.dram_tensor("xx", (BT, 2 * FIELDS, TPB, N), F32).ap()

        ids_all = sb("ids_all", [P, BT * FIELDS], I32)
        ids_now = sb("ids_now", [P, FIELDS], I32)
        emb = sb("emb", [P, FIELDS * E])
        ident = sb("ident", [P, P])
        xt = sb("xt", [P, N])
        x4 = sb("x4", [P, N])
        xr = sb("xr", [P, GC + 1, N])
        xb = sb("xb", [P, 2, 4, GC, N])
        z = sb("z", [P, ZSLOTS, GC, N])
        zh = sb("zh", [P, SSLOTS, GC, N], F32R)
        zl = sb("zl", [P, SSLOTS, GC, N], F32R)
        zrest = sb("zrest", [P, N], F32R)
        w_whole = sb("w_whole", [P, len(WHOLES), GC, P])
        w_hi = sb("w_hi", [P, len(SPLITS), GC, P], F32R)
        w_lo = sb("w_lo", [P, len(SPLITS), GC, P], F32R)
        w_rest = sb("w_rest", [P, P], F32R)
        keep01 = sb("keep01", [P, TPB * N])
        keep2 = sb("keep2", [P, TPB * N])
        bias = sb("bias", [P, 3])
        wt1 = sb("wt1", [P, 2, HID1])
        wt1_dense = sb("wt1_dense", [DENSE, HID1])
        wt2 = sb("wt2", [P, HID1 // P, HID2])
        wt3 = sb("wt3", [P, HID2 // P])
        bt1 = sb("bt1", [P, HID1 // P])
        bt2 = sb("bt2", [P, HID2 // P])
        dense = sb("dense", [DENSE, BATCH])
        sum01 = sb("sum01", [P, P])
        sum2 = sb("sum2", [P, P])
        hid1 = sb("hid1", [P, HID1 // P, P])
        hid2 = sb("hid2", [P, HID2 // P, P])
        y_row = sb("y_row", [1, BATCH])

        y = [bank(f"y{l}") for l in range(3)]
        h1 = bank("h1")
        h2 = [bank("h2a"), bank("h2b")]
        turn = [bank("turn0"), bank("turn1")]

        stage = z[:, 0:2, :, :].rearrange("p s c n -> p (s c n)").rearrange("p (k c n) -> p k c n", c=GC, n=P)
        stage_back = z[:, 2, 0, :].rearrange("p (c n) -> p c n", n=P)
        stage_rest = z[:, 2, 1, 0:P]

        s_ids = sem("s_ids")
        s_zero = sem("s_zero")
        s_weights = sem("s_weights")
        s_dense_weights = sem("s_dense_weights")
        s_ident = sem("s_ident")
        s_w_rounded = sem("s_w_rounded")
        s_w_ready = sem("s_w_ready")
        s_emb = sem("s_emb")
        s_turned = sem("s_turned")
        s_xt = sem("s_xt")
        s_xx = [sem(f"s_xx{k}") for k in range(TPB)]
        s_xr = sem("s_xr")
        s_xb = [[sem(f"s_xb{k}_{g}") for g in range(4)] for k in range(2)]
        s_z_ready = sem("s_z_ready")
        s_z_used = sem("s_z_used")
        s_zh = sem("s_zh")
        s_zl_pool = sem("s_zl_pool")
        s_zl_dve = sem("s_zl_dve")
        s_rest = sem("s_rest")
        s_rest_hi = sem("s_rest_hi")
        s_rest_ready = sem("s_rest_ready")
        s_y0 = sem("s_y0")
        s_relu = [sem(f"s_relu{l}") for l in range(3)]
        s_sum = [sem(f"s_sum{l}") for l in range(3)]
        s_top = [sem(f"s_top{l}") for l in range(3)]
        s_hid = [sem(f"s_hid{l}") for l in range(2)]
        s_row = sem("s_row")
        s_out = sem("s_out")

        block = ctx.enter_context(nc.Block())

        def number(i, q):
            return TPB * i + q

        @block.sync
        def _(sp):
            def store_x(bt):
                for k in range(TPB):
                    sp.wait_ge(s_xt, TPB * bt + k + 1)
                    for twice in range(2):
                        sp.dma_start(xx[bt, twice * FIELDS:(twice + 1) * FIELDS, k, :],
                                     xt[k * FIELDS:(k + 1) * FIELDS, :]).then_inc(s_xx[k], 16)

            def load_shifted(bt, k):
                sp.wait_ge(s_xx[k], 32 * bt + 32)
                for r in range(4):
                    rows = slice(r * FIELDS, (r + 1) * FIELDS)
                    for j in range(GC):
                        shift = 4 * j + r
                        sp.dma_start(xr[rows, j, :], xx[bt, shift:shift + FIELDS, k, :]).then_inc(s_xr, 16)
                    sp.dma_start(xr[rows, GC, :], xx[bt, REST:REST + FIELDS, k, :]).then_inc(s_xr, 16)
                    sp.dma_start(x4[rows, :], xx[bt, 0:FIELDS, k, :]).then_inc(s_xr, 16)

            def load_broadcast(bt, k, g):
                sp.wait_ge(s_xx[k], 32 * bt + 32)
                pairs = xx[bt, 0:FIELDS, k, :].rearrange("(j two) n -> two j n", two=2)
                for half in range(2):
                    sp.dma_start(xb[half * HALF:(half + 1) * HALF, k % 2, g, :, :],
                                 pairs[half, GC * g:GC * g + GC, :].partition_broadcast(HALF)
                                 ).then_inc(s_xb[k % 2][g], 16)

            sp.dma_start(ids_all[:, :], t["ids"]).then_inc(s_ids, 16)
            for n, key in enumerate(SPLITS):
                sp.dma_start(stage[:, n, :, :], t["w"][key]).then_inc(s_weights, 16)
            for n, key in enumerate(WHOLES):
                sp.dma_start(w_whole[:, n, :, :], t["w"][key]).then_inc(s_weights, 16)
            sp.dma_start(stage_back[FIELDS:P, 0, :], t["w0_back_first"]).then_inc(s_weights, 16)
            sp.dma_start(stage_back[:, 1:GC, :], t["w0_back"]).then_inc(s_weights, 16)
            for r in range(4):
                sp.dma_start(stage_rest[r * FIELDS:(r + 1) * FIELDS, :], t["w0_rest"]).then_inc(s_weights, 16)
            sp.dma_start(bias[:, :], t["bias"]).then_inc(s_weights, 16)
            for dst, src in ((wt1[:, :, :], t["wt1"]), (wt1_dense[:, :], t["wt1_dense"]), (wt2[:, :, :], t["wt2"]),
                             (wt3[:, :], t["wt3"]), (bt1[:, :], t["bt1"]), (bt2[:, :], t["bt2"]),
                             (dense[:, :], t["dense"])):
                sp.dma_start(dst, src).then_inc(s_dense_weights, 16)

            def round_(i, q):
                r = number(i, q)
                if q == 2 and exists(i + 1, 1, (1, 0)):
                    store_x(i + 1)
                if exists(i, q + 1, (0, 0)):
                    sp.wait_ge(s_rest_ready, r + 2)
                    load_shifted(i + (q + 2) // TPB, (q + 2) % TPB)
                if exists(i, q, (2, 0)) and exists(i, q, (0, 0)):
                    for g in range(4):
                        sp.wait_ge(s_z_ready, count(PLAN, i, q, (2, g)))
                        load_broadcast(*tile(i, q, 0), g)

            store_x(0)
            load_shifted(0, 0)
            for k in range(2):
                for g in range(4):
                    load_broadcast(0, k, g)
            peeled_rounds(sp, round_)
            sp.wait_ge(s_row, BT)
            sp.dma_start(out, y_row[:, :]).then_inc(s_out, 16)
            sp.wait_ge(s_out, 16)

        @block.gpsimd
        def _(pool):
            def gather(bt):
                if not isinstance(bt, int):
                    pool.wait_ge(s_turned, TPB * bt)
                pool.tensor_copy(ids_now[:, :], ids_all[:, bass.ts(bt, FIELDS)])
                pool.drain()
                for f in range(FIELDS):
                    pool.indirect_dma_start(
                        emb[:, f * E:(f + 1) * E], None, t["tables"][f],
                        bass.IndirectOffsetOnAxis(ap=ids_now[:, f:f + 1].bitcast(U32), axis=0)).then_inc(s_emb, 16)

            def round_(i, q):
                if q == 1 and not isinstance(i, int):
                    gather(i + 1)
                for key in BY_POOL[q]:
                    if not exists(i, q, key):
                        continue
                    pool.wait_ge(s_zh, count(SPLIT_OF, i, q, key))
                    if user := user_before(SPLIT_OF, SSLOTS, i, q, key):
                        pool.wait_ge(s_z_used, count(PLAN, *user))
                    s = sslot(q, key)
                    pool.tensor_tensor(zl[:, s, :, :], z[:, zslot(q, key), :, :], zh[:, s, :, :].bitcast(F32),
                                       ALU.subtract).then_inc(s_zl_pool, amount(BY_POOL, i, q, key))

            pool.memset(ident[:, :], 0.0).then_inc(s_ident, 1)
            pool.wait_ge(s_ids, 16)
            gather(0)
            pool.wait_ge(s_ident, 1)
            pool.affine_select(out=ident[:, :], in_=ident[:, :], compare_op=ALU.not_equal, fill=1.0, base=0,
                               pattern=[[-1, P]], channel_multiplier=1).then_inc(s_ident, 1)
            peeled_rounds(pool, round_)

        @block.scalar
        def _(act):
            def take_x(bt):
                for k in range(TPB):
                    if not isinstance(bt, int):
                        act.wait_ge(s_xx[k], 32 * bt)
                    act.wait_ge(s_turned, TPB * bt + k + 1)
                    act.activation(xt[k * FIELDS:(k + 1) * FIELDS, :], turn[k % 2][0:FIELDS, :],
                                   ACT.Copy).then_inc(s_xt, 1)

            def round_z(i, q, key):
                act.wait_ge(s_z_ready, count(PLAN, i, q, key))
                if user := user_before(SPLIT_OF, SSLOTS, i, q, key):
                    act.wait_ge(s_z_used, count(PLAN, *user))
                act.activation(zh[:, sslot(q, key), :, :], z[:, zslot(q, key), :, :],
                               ACT.Copy).then_inc(s_zh, amount(SPLIT_OF, i, q, key))

            def round_rest(c):
                act.wait_ge(s_rest, c + 1)
                if not (isinstance(c, int) and c == 0):
                    act.wait_ge(s_y0, c)
                act.activation(zrest[:, :], xr[:, GC, :], ACT.Copy).then_inc(s_rest_hi, 1)

            def relu(layer, i, q):
                bt, k = tile(i, q, layer)
                c = TPB * bt + k
                if layer == 0:
                    act.wait_ge(s_y0, c + 1)
                else:
                    act.wait_ge(s_z_used, count(PLAN, i, q, (layer, 3)))
                if k == 0 and not (isinstance(bt, int) and bt == 0):
                    act.wait_ge(s_sum[layer], bt)
                cols = slice(k * N, (k + 1) * N)
                if layer == 2:
                    act.activation(keep2[:, cols], y[2][:, :], ACT.Relu, bias=bias[:, 2:3]).then_inc(s_relu[2], 1)
                    return
                kept, passed = (slice(0, HALF), slice(HALF, P)) if layer == 0 else (slice(HALF, P), slice(0, HALF))
                if layer == 0 and exists(i, q, (1, 3)):
                    act.wait_ge(s_z_ready, count(PLAN, i, q, (1, 3)))
                if layer == 1 and (at := walk(PLAN, i, q, (1, 3), -PER)) and exists(*at[:2], (2, 3)):
                    act.wait_ge(s_z_ready, count(PLAN, *at[:2], (2, 3)))
                h = h1 if layer == 0 else h2[k % 2]
                for half in (slice(0, HALF), slice(HALF, P)):
                    act.activation(h[half, :], y[layer][passed, :], ACT.Relu,
                                   bias=bias[passed, layer:layer + 1]).then_inc(s_relu[layer], 1)
                act.activation(keep01[kept, cols], y[layer][kept, :], ACT.Relu,
                               bias=bias[kept, layer:layer + 1]).then_inc(s_relu[layer], 1)

            def dense_layers(bt):
                for layer, width, psum, hid, b in ((0, HID1, turn[0], hid1, bt1), (1, HID2, turn[1], hid2, bt2)):
                    act.wait_ge(s_top[layer], bt + 1)
                    for m in range(width // P):
                        act.activation(hid[:, m, :], psum[:, m * P:(m + 1) * P], ACT.Relu,
                                       bias=b[:, m:m + 1]).then_inc(s_hid[layer], 1)
                act.wait_ge(s_top[2], bt + 1)
                act.activation(y_row[:, bass.ts(bt, P)], turn[0][0:1, 0:P], ACT.Copy).then_inc(s_row, 1)

            late = []

            def round_(i, q):
                for key in PLAN[q]:
                    if not exists(i, q, key):
                        continue
                    if key == (0, 0):
                        round_rest(number(i, q) + 1)
                    if KIND[key] == SPLIT:
                        round_z(i, q, key)
                    while late:
                        late.pop(0)()
                    if key == (1, 3):
                        late.append(lambda: relu(1, i, q))
                    if key == (2, 3):
                        late.append(lambda: relu(2, i, q))
                    if key == (0, 0):
                        late.append(lambda: relu(0, i, q))
                        if q == 2 and not isinstance(i, int):
                            late.append(lambda: take_x(i + 1))
                        if q == 4 or opening(i):
                            late.pop(0)()
                if q == 4 or opening(i):
                    while late:
                        late.pop(0)()
                if q == 4 and not opening(i):
                    dense_layers(i)

            act.wait_ge(s_weights, 16 * (len(KIND) + 7))
            act.activation(w_hi[:, :, :, :], stage[:, 0:len(SPLITS), :, :], ACT.Copy).then_inc(s_w_rounded, 1)
            act.activation(w_rest[:, :], stage_rest, ACT.Copy).then_inc(s_w_rounded, 1)
            act.wait_ge(s_dense_weights, 16 * 7)
            take_x(0)
            peeled_rounds(act, round_)

        @block.vector
        def _(dve):
            def make_z(i, q, key):
                layer, g = key
                bt, k = tile(i, q, layer)
                c = TPB * bt + k
                if user := user_before(PLAN, ZSLOTS, i, q, key):
                    if KIND[user[2]] == WHOLE:
                        dve.wait_ge(s_z_used, count(PLAN, *user))
                    elif user[2] in BY_POOL[user[1]]:
                        dve.wait_ge(s_zl_pool, count(BY_POOL, *user))
                    else:
                        dve.wait_ge(s_zl_dve, count(BY_DVE, *user))
                if q == 1 and PLAN[q].index(key) < ZSLOTS:
                    at = walk(PLAN, i, q, PLAN[q][0], -1)[:2]
                    dve.wait_ge(s_z_used, count(PLAN, *at, (1, 3)))
                dst = z[:, zslot(q, key), :, :]
                if layer == 0:
                    dve.wait_ge(s_xr, 16 * 4 * (GC + 2) * (c + 1))
                    x = x4[:, :]
                    dve.tensor_tensor(dst, xr[:, 0:GC, :], x.unsqueeze(1).broadcast_to([P, GC, N]),
                                      ALU.mult).then_inc(s_z_ready, amount(PLAN, i, q, key))
                    dve.tensor_tensor(xr[:, GC, :], xr[:, GC, :], x, ALU.mult).then_inc(s_rest, 1)
                    return
                dve.wait_ge(s_relu[layer - 1], 3 * c + 2)
                if layer == 1:
                    dve.wait_ge(s_xb[k % 2][g], 32 * (TPB // 2 * bt + k // 2 + 1))
                h = h1 if layer == 1 else h2[k % 2]
                dve.tensor_tensor(dst, xb[:, k % 2, g, :, :], h[:, :].unsqueeze(1).broadcast_to([P, GC, N]),
                                  ALU.mult).then_inc(s_z_ready, amount(PLAN, i, q, key))

            def make_zl(i, q, key):
                dve.wait_ge(s_zh, count(SPLIT_OF, i, q, key))
                if user := user_before(SPLIT_OF, SSLOTS, i, q, key):
                    dve.wait_ge(s_z_used, count(PLAN, *user))
                s = sslot(q, key)
                dve.tensor_tensor(zl[:, s, :, :], z[:, zslot(q, key), :, :], zh[:, s, :, :].bitcast(F32),
                                  ALU.subtract).then_inc(s_zl_dve, amount(BY_DVE, i, q, key))

            def make_rest(c):
                dve.wait_ge(s_rest_hi, c + 1)
                dve.tensor_tensor(zrest[HALF:P, :], xr[HALF:P, GC, :], zrest[HALF:P, :].bitcast(F32),
                                  ALU.subtract).then_inc(s_rest_ready, 1)

            def sum_kept(layer, bt):
                kept, dst, rows = ((keep01, sum01, slice(0, HALF)), (keep01, sum01, slice(HALF, P)),
                                   (keep2, sum2, slice(0, P)))[layer]
                dve.wait_ge(s_relu[layer], (3, 3, 1)[layer] * TPB * (bt + 1))
                if not (isinstance(bt, int) and bt == 0):
                    dve.wait_ge(s_top[0], bt)
                dve.tensor_reduce(dst[rows, :], kept[rows, :].rearrange("p (e b) -> p b e", b=P), AX_X,
                                  ALU.add).then_inc(s_sum[layer], 1)

            late = []

            def round_(i, q):
                for key in PLAN[q]:
                    if not exists(i, q, key):
                        continue
                    make_z(i, q, key)
                    while late:
                        late.pop(0)()
                    if key in BY_DVE[q]:
                        late.append(lambda key=key: make_zl(i, q, key))
                    if key == (0, 0):
                        if q == 4 or opening(i):
                            make_rest(number(i, q) + 1)
                        else:
                            late.append(lambda: make_rest(number(i, q) + 1))
                while late:
                    late.pop(0)()
                if q >= 2 and not opening(i):
                    sum_kept(q - 2, i)

            dve.memset(stage_back[0:FIELDS, 0, :], 0.0).then_inc(s_zero, 1)
            dve.wait_ge(s_zero, 1)
            dve.wait_ge(s_weights, 16 * (len(KIND) + 7))
            folded = w_whole[:, WHOLES.index((0, 0)), :, :]
            dve.tensor_tensor(folded, folded, stage_back, ALU.add).then_inc(s_w_ready, 1)
            dve.wait_ge(s_w_rounded, 2)
            dve.tensor_tensor(w_lo[:, :, :, :], stage[:, 0:len(SPLITS), :, :], w_hi[:, :, :, :].bitcast(F32),
                              ALU.subtract).then_inc(s_w_ready, 1)
            for r in (1, 3):
                rows = slice(r * FIELDS, (r + 1) * FIELDS)
                dve.tensor_tensor(w_rest[rows, :], stage_rest[rows, :], w_rest[rows, :].bitcast(F32),
                                  ALU.subtract).then_inc(s_w_ready, 1)
            dve.wait_ge(s_w_ready, 4)
            peeled_rounds(dve, round_)

        @block.tensor
        def _(pe):
            def turn_x(bt):
                pe.wait_ge(s_emb, 16 * FIELDS * (bt + 1))
                if not isinstance(bt, int):
                    pe.wait_ge(s_row, bt - 1)
                for k in range(TPB):
                    if k >= 2 or not isinstance(bt, int):
                        pe.wait_ge(s_xt, TPB * bt + k - 1)
                    for n in range(EQ):
                        rows = emb[:, :].rearrange("b (f e) -> b e f", e=E)[:, EQ * k + n, :]
                        step = pe.transpose(turn[k % 2][0:FIELDS, n * P:(n + 1) * P], rows, ident[:, :])
                    step.then_inc(s_turned, 1)

            def multiply(i, q, key):
                layer, g = key
                bt, k = tile(i, q, layer)
                c = TPB * bt + k
                acc, last = y[layer][:, :], g == 3
                if g == 0 and not (isinstance(c, int) and c == 0):
                    pe.wait_ge(s_relu[layer], (3, 3, 1)[layer] * c)
                if KIND[key] == WHOLE:
                    w, zs = w_whole[:, WHOLES.index(key), :, :], z[:, zslot(q, key), :, :]
                    pe.wait_ge(s_z_ready, count(PLAN, i, q, key))
                    for j in range(GC):
                        step = pe.matmul(acc, w[:, j, :], zs[:, j, :], start=g == 0 and j == 0, stop=last and j == GC - 1)
                else:
                    n, s = SPLITS.index(key), sslot(q, key)
                    pe.wait_ge(s_zh, count(SPLIT_OF, i, q, key))
                    for j in range(GC):
                        pe.matmul(acc, w_hi[:, n, j, :], zh[:, s, j, :], start=g == 0 and j == 0, stop=False)
                        pe.matmul(acc, w_lo[:, n, j, :], zh[:, s, j, :], start=False, stop=False)
                    if key in BY_POOL[q]:
                        pe.wait_ge(s_zl_pool, count(BY_POOL, i, q, key))
                    else:
                        pe.wait_ge(s_zl_dve, count(BY_DVE, i, q, key))
                    for j in range(GC):
                        step = pe.matmul(acc, w_hi[:, n, j, :], zl[:, s, j, :], start=False, stop=last and j == GC - 1)
                step.then_inc(s_z_used, amount(PLAN, i, q, key))
                if layer == 0:
                    pe.wait_ge(s_rest_ready, c + 1)
                    pe.matmul(acc, w_rest[:, :], zrest[:, :], start=False, stop=True).then_inc(s_y0, 1)

            def dense_layers(bt):
                for layer in range(3):
                    pe.wait_ge(s_sum[layer], bt + 1)
                if isinstance(bt, int):
                    pe.wait_ge(s_xt, CT)
                else:
                    pe.wait_ge(s_xt, TPB * (bt + 2))
                for m in range(HID1 // P):
                    cols = slice(m * P, (m + 1) * P)
                    pe.matmul(turn[0][:, cols], wt1[:, 0, cols], sum01[:, :], start=True, stop=False)
                    pe.matmul(turn[0][:, cols], wt1[:, 1, cols], sum2[:, :], start=False, stop=False)
                    step = pe.matmul(turn[0][:, cols], wt1_dense[:, cols], dense[:, bass.ts(bt, P)],
                                     start=False, stop=True)
                step.then_inc(s_top[0], 1)
                pe.wait_ge(s_hid[0], HID1 // P * (bt + 1))
                for m in range(HID2 // P):
                    cols = slice(m * P, (m + 1) * P)
                    for n in range(HID1 // P):
                        step = pe.matmul(turn[1][:, cols], wt2[:, n, cols], hid1[:, n, :], start=n == 0,
                                         stop=n == HID1 // P - 1)
                step.then_inc(s_top[1], 1)
                pe.wait_ge(s_hid[1], HID2 // P * (bt + 1))
                for n in range(HID2 // P):
                    step = pe.matmul(turn[0][0:1, 0:P], wt3[:, n:n + 1], hid2[:, n, :], start=n == 0,
                                     stop=n == HID2 // P - 1)
                step.then_inc(s_top[2], 1)

            def round_(i, q):
                for key in PLAN[q]:
                    if not exists(i, q, key):
                        continue
                    multiply(i, q, key)
                    if key == (0, 0) and q == 2 and not isinstance(i, int):
                        turn_x(i + 1)
                if q == 4 and not opening(i):
                    dense_layers(i)

            pe.wait_ge(s_ident, 2)
            turn_x(0)
            pe.wait_ge(s_w_ready, 4)
            pe.wait_ge(s_dense_weights, 16 * 7)
            peeled_rounds(pe, round_)


def kernel(**inputs):
    import numpy as np
    import concourse.bacc as bacc
    from concourse.bass_utils import run_bass_kernel_spmd

    a = {name: np.asarray(value) for name, value in inputs.items()}
    nc = bacc.Bacc("TRN2", target_bir_lowering=False, num_devices=1)
    arrays = {}

    def give(name, value):
        name = f"in_{name}"
        arrays[name] = np.ascontiguousarray(value)
        return nc.dram_tensor(name, arrays[name].shape, mybir.dt.from_np(arrays[name].dtype), kind="ExternalInput").ap()

    def pairs(w, swap):
        rows = w.T if not swap else np.concatenate([w.T[:, HALF:], w.T[:, :HALF]], axis=1)
        return rows.reshape(4, GC, P, P).transpose(0, 2, 1, 3)

    w0 = a["L0_rec_W0"].reshape(P, FIELDS, FIELDS).transpose(1, 2, 0)
    f = np.arange(FIELDS)
    fg = np.stack([w0[f, (f + k) % FIELDS] for k in range(REST)])
    gf = np.stack([w0[(f + k) % FIELDS, f] for k in range(REST)])
    as_chunks = lambda x: x.reshape(GC, P, P).transpose(1, 0, 2)
    w1, w2 = pairs(a["L0_rec_W1"], True), pairs(a["L0_rec_W2"], False)
    b1 = a["L0_rec_b1"]
    t = {
        "tables": [give(f"tbl_{n}", a[f"tbl_{n}"]) for n in range(FIELDS)],
        "ids": give("ids", a["ids"].reshape(BT, P, FIELDS).transpose(1, 0, 2).reshape(P, BT * FIELDS)),
        "w": {(0, 0): give("w0", as_chunks(fg)),
              **{(1, g): give(f"w1_{g}", w1[g]) for g in range(4)},
              **{(2, g): give(f"w2_{g}", w2[g]) for g in range(4)}},
        "w0_back_first": give("w0_back_first", as_chunks(gf)[FIELDS:, 0]),
        "w0_back": give("w0_back", as_chunks(gf)[:, 1:]),
        "w0_rest": give("w0_rest", w0[f, (f + REST) % FIELDS]),
        "bias": give("bias", np.stack([a["L0_rec_b0"], np.concatenate([b1[HALF:], b1[:HALF]]), a["L0_rec_b2"]], axis=1)),
        "wt1": give("wt1", a["W_top1"][:2 * P].reshape(2, P, HID1).transpose(1, 0, 2)),
        "wt1_dense": give("wt1_dense", a["W_top1"][2 * P:]),
        "wt2": give("wt2", a["W_top2"].reshape(HID1 // P, P, HID2).transpose(1, 0, 2)),
        "wt3": give("wt3", a["W_top3"].reshape(HID2 // P, P).T),
        "bt1": give("bt1", a["b_top1"].reshape(HID1 // P, P).T),
        "bt2": give("bt2", a["b_top2"].reshape(HID2 // P, P).T),
        "dense": give("dense", a["dense_ctx"].T),
    }
    out = nc.dram_tensor("out", (BATCH, 1), F32, kind="ExternalOutput").ap()
    cin_tower(nc, t, out.rearrange("b one -> one b"))
    result = run_bass_kernel_spmd(nc, [arrays], core_ids=[0])
    return result.results[0]["out"]
```

```python
from contextlib import ExitStack

import concourse.bass as bass
from concourse import mybir

F32 = mybir.dt.float32
F32R = mybir.dt.float32r
I32 = mybir.dt.int32
U32 = mybir.dt.uint32
ALU = mybir.AluOpType
ACT = mybir.ActivationFunctionType
AX_X = mybir.AxisListType.X

P = 128
FIELDS, E, BATCH, DENSE = 32, 16, 512, 16
HALF = 64
HID1, HID2 = 512, 256
BT = BATCH // P
EQ = 4
TPB = E // EQ
CT = BT * TPB
N = EQ * P
GC = 2
RELU_BEHIND = 3
COPIES = 5
LC = 4
ZSLOTS, SSLOTS = 6, 4
REST = FIELDS // 2
SHIFTED = REST * FIELDS // P

WHOLE, SPLIT = "whole", "split"
KIND = {(0, g): WHOLE for g in range(4 // GC)}
KIND |= {(layer, g): WHOLE if g in (3, 7) else SPLIT for layer in (1, 2) for g in range(16 // GC)}
SPLITS = [k for k in KIND if KIND[k] == SPLIT]
WHOLES = [k for k in KIND if KIND[k] == WHOLE]

L0, L1, L2 = ([k for k in KIND if k[0] == layer] for layer in range(3))
END = {layer: [k for k in KIND if k[0] == layer][-1] for layer in range(3)}

PLAN = {q: L1 + L2 + L0 if q == 4 else L1 + L0 + L2 for q in range(1, 5)}
SPLIT_OF = {q: [k for k in PLAN[q] if KIND[k] == SPLIT] for q in PLAN}
BY_POOL = {q: [k for k in SPLIT_OF[q] if q != 1] for q in PLAN}
BY_DVE = {q: [k for k in SPLIT_OF[q] if k not in BY_POOL[q]] for q in PLAN}
PER = len(PLAN[1])
assert PER % ZSLOTS == 0 and len(SPLITS) % SSLOTS == 0 and all(KIND[k] == WHOLE for k in L0)


def tile(i, q, layer):
    n = q + (1, 0, -1)[layer]
    return i + n // TPB, n % TPB


def opening(i):
    return isinstance(i, int) and i < 0


def exists(i, q, key):
    return not isinstance(i, int) or 0 <= TPB * i + q + (1, 0, -1)[key[0]] < CT


def walk(members, i, q, key, step):
    n = members[q].index(key) + step
    while n < 0:
        i, q = (i - 1, 4) if q == 1 else (i, q - 1)
        n += len(members[q])
    while n >= len(members[q]):
        n -= len(members[q])
        i, q = (i + 1, 1) if q == 4 else (i, q + 1)
    return i, q, members[q][n]


def place(members, i, q, key):
    return (i + 1) * sum(map(len, members.values())) + sum(len(members[k]) for k in range(1, q)) + members[q].index(key)


def first(members):
    return min(place(members, i, q, k) for i in (-1, 0) for q in members for k in members[q] if exists(i, q, k))


def count(members, i, q, key):
    return place(members, i, q, key) - first(members) + 1


def amount(members, i, q, key):
    n = 1
    while isinstance(i, int) and not exists(*(at := walk(members, i, q, key, n))) and at[0] < BT:
        n += 1
    return n


def user_before(members, ring, i, q, key):
    at = walk(members, i, q, key, -ring)
    while not exists(*at):
        if isinstance(at[0], int) and at[0] < -1:
            return None
        at = walk(members, *at, -ring)
    return at


def zslot(q, key):
    return PLAN[q].index(key) % ZSLOTS


def sslot(q, key):
    return place(SPLIT_OF, 0, q, key) % SSLOTS


def peeled_rounds(engine, round_):
    for q in (3, 4):
        round_(-1, q)
    with engine.Fori(0, BT - 1) as i:
        for q in range(1, 5):
            round_(i, q)
    for q in range(1, 5):
        round_(BT - 1, q)


def cin_tower(nc, t, out):
    with ExitStack() as ctx:
        def sb(name, shape, dt=F32):
            return ctx.enter_context(nc.sbuf_tensor(name, shape, dt))

        def bank(name, dt=F32):
            return ctx.enter_context(nc.psum_tensor(name, [P, N], dt))

        def sem(name):
            return ctx.enter_context(nc.semaphore(name))

        xx = nc.dram_tensor("xx", (BT, COPIES * FIELDS, TPB, N), F32).ap()

        ids_all = sb("ids_all", [P, BT * FIELDS], I32)
        ids_now = sb("ids_now", [P, FIELDS], I32)
        emb = sb("emb", [P, FIELDS * E])
        ident = sb("ident", [P, P])
        xt = sb("xt", [P, N])
        xs = sb("xs", [P, SHIFTED + 2, N])
        xb = sb("xb", [P, 2, FIELDS // 2, N])
        z = sb("z", [P, ZSLOTS, GC, N])
        zh = sb("zh", [P, SSLOTS, GC, N], F32R)
        zl = sb("zl", [P, SSLOTS, GC, N], F32R)
        zrest = sb("zrest", [P, N], F32R)
        w_whole = sb("w_whole", [P, len(WHOLES), GC, P])
        w_hi = sb("w_hi", [P, len(SPLITS), GC, P], F32R)
        w_lo = sb("w_lo", [P, len(SPLITS), GC, P], F32R)
        w_rest = sb("w_rest", [P, P], F32R)
        keep01 = sb("keep01", [P, TPB * N])
        keep2 = sb("keep2", [P, TPB * N])
        bias = sb("bias", [P, 3])
        wt1 = sb("wt1", [P, 2, HID1])
        wt1_dense = sb("wt1_dense", [DENSE, HID1])
        wt2 = sb("wt2", [P, HID1 // P, HID2])
        wt3 = sb("wt3", [P, HID2 // P])
        bt1 = sb("bt1", [P, HID1 // P])
        bt2 = sb("bt2", [P, HID2 // P])
        dense = sb("dense", [DENSE, BATCH])
        sum01 = sb("sum01", [P, P])
        sum2 = sb("sum2", [P, P])
        hid1 = sb("hid1", [P, HID1 // P, P])
        hid2 = sb("hid2", [P, HID2 // P, P])
        y_row = sb("y_row", [1, BATCH])

        y = [bank(f"y{l}") for l in range(3)]
        h1 = bank("h1")
        h2 = [bank("h2a"), bank("h2b")]
        turn = [bank("turn0"), bank("turn1")]

        stage_all = z[:, :, :, :].rearrange("p s c n -> p (s c n)").rearrange("p (k n) -> p k n", n=P)
        stage = stage_all[:, 0:GC * len(SPLITS), :].rearrange("p (k c) n -> p k c n", c=GC)
        stage_back = stage_all[:, GC * len(SPLITS):GC * len(SPLITS) + SHIFTED, :]
        stage_rest = stage_all[:, GC * len(SPLITS) + SHIFTED, :]

        s_ids = sem("s_ids")
        s_zero = sem("s_zero")
        s_weights = sem("s_weights")
        s_dense_weights = sem("s_dense_weights")
        s_ident = sem("s_ident")
        s_w_rounded = sem("s_w_rounded")
        s_w_ready = sem("s_w_ready")
        s_emb = sem("s_emb")
        s_turned = sem("s_turned")
        s_xt = sem("s_xt")
        s_xx = [sem(f"s_xx{k}") for k in range(TPB)]
        s_xs = sem("s_xs")
        s_xb = [[sem(f"s_xb{k}_{g}") for g in range(16 // LC)] for k in range(2)]
        s_z_ready = sem("s_z_ready")
        s_z_used = sem("s_z_used")
        s_zh = sem("s_zh")
        s_zl_pool = sem("s_zl_pool")
        s_zl_dve = sem("s_zl_dve")
        s_rest = sem("s_rest")
        s_rest_hi = sem("s_rest_hi")
        s_rest_ready = sem("s_rest_ready")
        s_y0 = sem("s_y0")
        s_relu = [sem(f"s_relu{l}") for l in range(3)]
        s_sum = [sem(f"s_sum{l}") for l in range(3)]
        s_top = [sem(f"s_top{l}") for l in range(3)]
        s_hid = [sem(f"s_hid{l}") for l in range(2)]
        s_row = sem("s_row")
        s_out = sem("s_out")

        block = ctx.enter_context(nc.Block())

        def number(i, q):
            return TPB * i + q

        @block.sync
        def _(sp):
            def store_x(bt):
                for k in range(TPB):
                    sp.wait_ge(s_xt, TPB * bt + k + 1)
                    sp.dma_start(xx[bt, :, k, :].rearrange("(c f) n -> f c n", f=FIELDS),
                                 xt[k * FIELDS:(k + 1) * FIELDS, :].unsqueeze(1).broadcast_to([FIELDS, COPIES, N])
                                 ).then_inc(s_xx[k], 16)

            def load_shifted(bt, k):
                sp.wait_ge(s_xx[k], 16 * bt + 16)
                sp.dma_start(xs[:, SHIFTED:, :], rows_from(bt, 0, k, P, REST, 2)).then_inc(s_xs, 16)
                for r in range(4):
                    sp.dma_start(xs[r * FIELDS:(r + 1) * FIELDS, 0:SHIFTED, :],
                                 rows_from(bt, r, k, FIELDS, 4, SHIFTED)).then_inc(s_xs, 16)

            def rows_from(bt, row, k, parts, step, chunks):
                start = xx[bt, row:row + 1, k, :]
                return bass.AP(start.tensor, start.offset, [[TPB * N, parts], [step * TPB * N, chunks], [1, N]])

            def load_broadcast(bt, k, g):
                sp.wait_ge(s_xx[k], 16 * bt + 16)
                pairs = xx[bt, 0:FIELDS, k, :].rearrange("(j two) n -> two j n", two=2)
                for half in range(2):
                    sp.dma_start(xb[half * HALF:(half + 1) * HALF, k % 2, LC * g:LC * g + LC, :],
                                 pairs[half, LC * g:LC * g + LC, :].partition_broadcast(HALF)
                                 ).then_inc(s_xb[k % 2][g], 16)

            sp.dma_start(ids_all[:, :], t["ids"]).then_inc(s_ids, 16)
            for n, key in enumerate(SPLITS):
                sp.dma_start(stage[:, n, :, :], t["w"][key]).then_inc(s_weights, 16)
            for n, key in enumerate(WHOLES):
                sp.dma_start(w_whole[:, n, :, :], t["w"][key]).then_inc(s_weights, 16)
            sp.dma_start(stage_back[FIELDS:P, 0, :], t["w0_back_first"]).then_inc(s_weights, 16)
            sp.dma_start(stage_back[:, 1:SHIFTED, :], t["w0_back"]).then_inc(s_weights, 16)
            for r in range(4):
                sp.dma_start(stage_rest[r * FIELDS:(r + 1) * FIELDS, :], t["w0_rest"]).then_inc(s_weights, 16)
            sp.dma_start(bias[:, :], t["bias"]).then_inc(s_weights, 16)
            for dst, src in ((wt1[:, :, :], t["wt1"]), (wt1_dense[:, :], t["wt1_dense"]), (wt2[:, :, :], t["wt2"]),
                             (wt3[:, :], t["wt3"]), (bt1[:, :], t["bt1"]), (bt2[:, :], t["bt2"]),
                             (dense[:, :], t["dense"])):
                sp.dma_start(dst, src).then_inc(s_dense_weights, 16)

            def round_(i, q):
                r = number(i, q)

                def shifted():
                    if exists(i, q + 1, (0, 0)):
                        sp.wait_ge(s_rest_ready, r + 2)
                        load_shifted(i + (q + 2) // TPB, (q + 2) % TPB)

                if q != 2:
                    shifted()
                if exists(i, q, (2, 0)) and exists(i, q, (0, 0)):
                    for g in range(16 // LC):
                        sp.wait_ge(s_z_ready, count(PLAN, i, q, (2, LC // GC * (g + 1) - 1)))
                        load_broadcast(*tile(i, q, 0), g)
                if q == 2:
                    if exists(i + 1, 1, (1, 0)):
                        store_x(i + 1)
                    shifted()

            store_x(0)
            load_shifted(0, 0)
            for k in range(2):
                for g in range(16 // LC):
                    load_broadcast(0, k, g)
            peeled_rounds(sp, round_)
            sp.wait_ge(s_row, BT)
            sp.dma_start(out, y_row[:, :]).then_inc(s_out, 16)
            sp.wait_ge(s_out, 16)

        @block.gpsimd
        def _(pool):
            def gather(bt):
                if not isinstance(bt, int):
                    pool.wait_ge(s_turned, TPB * bt)
                pool.tensor_copy(ids_now[:, :], ids_all[:, bass.ts(bt, FIELDS)])
                pool.drain()
                for f in range(FIELDS):
                    pool.indirect_dma_start(
                        emb[:, f * E:(f + 1) * E], None, t["tables"][f],
                        bass.IndirectOffsetOnAxis(ap=ids_now[:, f:f + 1].bitcast(U32), axis=0)).then_inc(s_emb, 16)

            def round_(i, q):
                if q == 1 and not isinstance(i, int):
                    gather(i + 1)
                for key in BY_POOL[q]:
                    if not exists(i, q, key):
                        continue
                    pool.wait_ge(s_zh, count(SPLIT_OF, i, q, key))
                    if user := user_before(SPLIT_OF, SSLOTS, i, q, key):
                        pool.wait_ge(s_z_used, count(PLAN, *user))
                    s = sslot(q, key)
                    pool.tensor_tensor(zl[:, s, :, :], z[:, zslot(q, key), :, :], zh[:, s, :, :].bitcast(F32),
                                       ALU.subtract).then_inc(s_zl_pool, amount(BY_POOL, i, q, key))

            pool.memset(ident[:, :], 0.0).then_inc(s_ident, 1)
            pool.wait_ge(s_ids, 16)
            gather(0)
            pool.wait_ge(s_ident, 1)
            pool.affine_select(out=ident[:, :], in_=ident[:, :], compare_op=ALU.not_equal, fill=1.0, base=0,
                               pattern=[[-1, P]], channel_multiplier=1).then_inc(s_ident, 1)
            peeled_rounds(pool, round_)

        @block.scalar
        def _(act):
            def take_x(bt):
                for k in range(TPB):
                    if not isinstance(bt, int):
                        act.wait_ge(s_xx[k], 16 * bt)
                    act.wait_ge(s_turned, TPB * bt + k + 1)
                    act.activation(xt[k * FIELDS:(k + 1) * FIELDS, :], turn[k % 2][0:FIELDS, :],
                                   ACT.Copy).then_inc(s_xt, 1)

            def round_z(i, q, key):
                act.wait_ge(s_z_ready, count(PLAN, i, q, key))
                if user := user_before(SPLIT_OF, SSLOTS, i, q, key):
                    act.wait_ge(s_z_used, count(PLAN, *user))
                act.activation(zh[:, sslot(q, key), :, :], z[:, zslot(q, key), :, :],
                               ACT.Copy).then_inc(s_zh, amount(SPLIT_OF, i, q, key))

            def round_rest(c):
                act.wait_ge(s_rest, c + 1)
                if not (isinstance(c, int) and c == 0):
                    act.wait_ge(s_y0, c)
                act.activation(zrest[:, :], xs[:, SHIFTED + 1, :], ACT.Copy).then_inc(s_rest_hi, 1)

            def relu(layer, i, q):
                bt, k = tile(i, q, layer)
                c = TPB * bt + k
                if layer == 0:
                    act.wait_ge(s_y0, c + 1)
                else:
                    act.wait_ge(s_z_used, count(PLAN, i, q, END[layer]))
                if k == 0 and not (isinstance(bt, int) and bt == 0):
                    act.wait_ge(s_sum[layer], bt)
                cols = slice(k * N, (k + 1) * N)
                if layer == 2:
                    act.activation(keep2[:, cols], y[2][:, :], ACT.Relu, bias=bias[:, 2:3]).then_inc(s_relu[2], 1)
                    return
                kept, passed = (slice(0, HALF), slice(HALF, P)) if layer == 0 else (slice(HALF, P), slice(0, HALF))
                if layer == 0 and exists(i, q, END[1]):
                    act.wait_ge(s_z_ready, count(PLAN, i, q, END[1]))
                if layer == 1 and (at := walk(PLAN, i, q, END[1], -PER)) and exists(*at[:2], END[2]):
                    act.wait_ge(s_z_ready, count(PLAN, *at[:2], END[2]))
                h = h1 if layer == 0 else h2[k % 2]
                for half in (slice(0, HALF), slice(HALF, P)):
                    act.activation(h[half, :], y[layer][passed, :], ACT.Relu,
                                   bias=bias[passed, layer:layer + 1]).then_inc(s_relu[layer], 1)
                act.activation(keep01[kept, cols], y[layer][kept, :], ACT.Relu,
                               bias=bias[kept, layer:layer + 1]).then_inc(s_relu[layer], 1)

            def dense_layers(bt):
                for layer, width, psum, hid, b in ((0, HID1, turn[0], hid1, bt1), (1, HID2, turn[1], hid2, bt2)):
                    act.wait_ge(s_top[layer], bt + 1)
                    for m in range(width // P):
                        act.activation(hid[:, m, :], psum[:, m * P:(m + 1) * P], ACT.Relu,
                                       bias=b[:, m:m + 1]).then_inc(s_hid[layer], 1)
                act.wait_ge(s_top[2], bt + 1)
                act.activation(y_row[:, bass.ts(bt, P)], turn[0][0:1, 0:P], ACT.Copy).then_inc(s_row, 1)

            late = []

            def flush(all_=False):
                while late and (all_ or late[0][0] <= 0):
                    late.pop(0)[1]()

            def round_(i, q):
                for key in PLAN[q]:
                    if not exists(i, q, key):
                        continue
                    if key == END[0]:
                        round_rest(number(i, q) + 1)
                    if KIND[key] == SPLIT:
                        round_z(i, q, key)
                    for entry in late:
                        entry[0] -= 1
                    flush()
                    if key == END[key[0]]:
                        late.append([RELU_BEHIND, lambda layer=key[0]: relu(layer, i, q)])
                    if key == END[0] and q == 2 and not isinstance(i, int):
                        late.append([RELU_BEHIND, lambda: take_x(i + 1)])
                    if key == END[0] and (q == 4 or opening(i)):
                        flush(True)
                if q == 4 or opening(i):
                    flush(True)
                if q == 4 and not opening(i):
                    dense_layers(i)

            act.wait_ge(s_weights, 16 * (len(KIND) + 7))
            act.activation(w_hi[:, :, :, :], stage[:, 0:len(SPLITS), :, :], ACT.Copy).then_inc(s_w_rounded, 1)
            act.activation(w_rest[:, :], stage_rest, ACT.Copy).then_inc(s_w_rounded, 1)
            act.wait_ge(s_dense_weights, 16 * 7)
            take_x(0)
            peeled_rounds(act, round_)

        @block.vector
        def _(dve):
            def make_z(i, q, key):
                layer, g = key
                bt, k = tile(i, q, layer)
                c = TPB * bt + k
                if user := user_before(PLAN, ZSLOTS, i, q, key):
                    if KIND[user[2]] == WHOLE:
                        dve.wait_ge(s_z_used, count(PLAN, *user))
                    elif user[2] in BY_POOL[user[1]]:
                        dve.wait_ge(s_zl_pool, count(BY_POOL, *user))
                    else:
                        dve.wait_ge(s_zl_dve, count(BY_DVE, *user))
                if q == 1 and PLAN[q].index(key) < ZSLOTS:
                    at = walk(PLAN, i, q, PLAN[q][0], -1)[:2]
                    dve.wait_ge(s_z_used, count(PLAN, *at, END[1]))
                dst = z[:, zslot(q, key), :, :]
                if layer == 0:
                    dve.wait_ge(s_xs, 16 * 5 * (c + 1))
                    x = xs[:, SHIFTED, :]
                    dve.tensor_tensor(dst, xs[:, GC * g:GC * g + GC, :], x.unsqueeze(1).broadcast_to([P, GC, N]),
                                      ALU.mult).then_inc(s_z_ready, amount(PLAN, i, q, key))
                    if key == END[0]:
                        dve.tensor_tensor(xs[:, SHIFTED + 1, :], xs[:, SHIFTED + 1, :], x, ALU.mult).then_inc(s_rest, 1)
                    return
                dve.wait_ge(s_relu[layer - 1], 3 * c + 2)
                if layer == 1:
                    dve.wait_ge(s_xb[k % 2][GC * g // LC], 32 * (TPB // 2 * bt + k // 2 + 1))
                h = h1 if layer == 1 else h2[k % 2]
                dve.tensor_tensor(dst, xb[:, k % 2, GC * g:GC * g + GC, :], h[:, :].unsqueeze(1).broadcast_to([P, GC, N]),
                                  ALU.mult).then_inc(s_z_ready, amount(PLAN, i, q, key))

            def make_zl(i, q, key):
                dve.wait_ge(s_zh, count(SPLIT_OF, i, q, key))
                if user := user_before(SPLIT_OF, SSLOTS, i, q, key):
                    dve.wait_ge(s_z_used, count(PLAN, *user))
                s = sslot(q, key)
                dve.tensor_tensor(zl[:, s, :, :], z[:, zslot(q, key), :, :], zh[:, s, :, :].bitcast(F32),
                                  ALU.subtract).then_inc(s_zl_dve, amount(BY_DVE, i, q, key))

            def make_rest(c):
                dve.wait_ge(s_rest_hi, c + 1)
                dve.tensor_tensor(zrest[HALF:P, :], xs[HALF:P, SHIFTED + 1, :], zrest[HALF:P, :].bitcast(F32),
                                  ALU.subtract).then_inc(s_rest_ready, 1)

            def sum_kept(layer, bt):
                kept, dst, rows = ((keep01, sum01, slice(0, HALF)), (keep01, sum01, slice(HALF, P)),
                                   (keep2, sum2, slice(0, P)))[layer]
                dve.wait_ge(s_relu[layer], (3, 3, 1)[layer] * TPB * (bt + 1))
                if not (isinstance(bt, int) and bt == 0):
                    dve.wait_ge(s_top[0], bt)
                dve.tensor_reduce(dst[rows, :], kept[rows, :].rearrange("p (e b) -> p b e", b=P), AX_X,
                                  ALU.add).then_inc(s_sum[layer], 1)

            late = []

            def round_(i, q):
                for key in PLAN[q]:
                    if not exists(i, q, key):
                        continue
                    make_z(i, q, key)
                    while late:
                        late.pop(0)()
                    if key in BY_DVE[q]:
                        late.append(lambda key=key: make_zl(i, q, key))
                    if key == END[0]:
                        if q == 4 or opening(i):
                            make_rest(number(i, q) + 1)
                        else:
                            late.append(lambda: make_rest(number(i, q) + 1))
                while late:
                    late.pop(0)()
                if q >= 2 and not opening(i):
                    sum_kept(q - 2, i)

            dve.memset(stage_back[0:FIELDS, 0, :], 0.0).then_inc(s_zero, 1)
            dve.wait_ge(s_zero, 1)
            dve.wait_ge(s_weights, 16 * (len(KIND) + 7))
            folded = w_whole[:, 0:len(L0), :, :].rearrange("p g c n -> p (g c) n")
            dve.tensor_tensor(folded, folded, stage_back, ALU.add).then_inc(s_w_ready, 1)
            dve.wait_ge(s_w_rounded, 2)
            dve.tensor_tensor(w_lo[:, :, :, :], stage[:, 0:len(SPLITS), :, :], w_hi[:, :, :, :].bitcast(F32),
                              ALU.subtract).then_inc(s_w_ready, 1)
            for r in (1, 3):
                rows = slice(r * FIELDS, (r + 1) * FIELDS)
                dve.tensor_tensor(w_rest[rows, :], stage_rest[rows, :], w_rest[rows, :].bitcast(F32),
                                  ALU.subtract).then_inc(s_w_ready, 1)
            dve.wait_ge(s_w_ready, 4)
            peeled_rounds(dve, round_)

        @block.tensor
        def _(pe):
            def turn_x(bt):
                pe.wait_ge(s_emb, 16 * FIELDS * (bt + 1))
                if not isinstance(bt, int):
                    pe.wait_ge(s_row, bt - 1)
                for k in range(TPB):
                    if k >= 2 or not isinstance(bt, int):
                        pe.wait_ge(s_xt, TPB * bt + k - 1)
                    for n in range(EQ):
                        rows = emb[:, :].rearrange("b (f e) -> b e f", e=E)[:, EQ * k + n, :]
                        step = pe.transpose(turn[k % 2][0:FIELDS, n * P:(n + 1) * P], rows, ident[:, :])
                    step.then_inc(s_turned, 1)

            late = []

            def multiply(i, q, key):
                layer, g = key
                bt, k = tile(i, q, layer)
                c = TPB * bt + k
                acc = y[layer][:, :]
                if g == 0 and not (isinstance(c, int) and c == 0):
                    pe.wait_ge(s_relu[layer], (3, 3, 1)[layer] * c)
                if KIND[key] == WHOLE:
                    w, zs = w_whole[:, WHOLES.index(key), :, :], z[:, zslot(q, key), :, :]
                    pe.wait_ge(s_z_ready, count(PLAN, i, q, key))
                    for j in range(GC):
                        if j == GC - 1 and late:
                            late.pop(0)()
                        step = pe.matmul(acc, w[:, j, :], zs[:, j, :], start=g == 0 and j == 0,
                                         stop=layer > 0 and key == END[layer] and j == GC - 1)
                    step.then_inc(s_z_used, amount(PLAN, i, q, key))
                else:
                    n, s = SPLITS.index(key), sslot(q, key)
                    pe.wait_ge(s_zh, count(SPLIT_OF, i, q, key))
                    for j in range(GC):
                        pe.matmul(acc, w_hi[:, n, j, :], zh[:, s, j, :], start=g == 0 and j == 0, stop=False)
                        pe.matmul(acc, w_lo[:, n, j, :], zh[:, s, j, :], start=False, stop=False)
                    if late:
                        late.pop(0)()

                    def lower():
                        if key in BY_POOL[q]:
                            pe.wait_ge(s_zl_pool, count(BY_POOL, i, q, key))
                        else:
                            pe.wait_ge(s_zl_dve, count(BY_DVE, i, q, key))
                        for j in range(GC):
                            step = pe.matmul(acc, w_hi[:, n, j, :], zl[:, s, j, :], start=False,
                                             stop=key == END[layer] and j == GC - 1)
                        step.then_inc(s_z_used, amount(PLAN, i, q, key))
                    late.append(lower)
                if key == END[layer] and late:
                    late.pop(0)()
                if key == END[0]:
                    pe.wait_ge(s_rest_ready, c + 1)
                    pe.matmul(acc, w_rest[:, :], zrest[:, :], start=False, stop=True).then_inc(s_y0, 1)

            def dense_layers(bt):
                for layer in range(3):
                    pe.wait_ge(s_sum[layer], bt + 1)
                if isinstance(bt, int):
                    pe.wait_ge(s_xt, CT)
                else:
                    pe.wait_ge(s_xt, TPB * (bt + 2))
                for m in range(HID1 // P):
                    cols = slice(m * P, (m + 1) * P)
                    pe.matmul(turn[0][:, cols], wt1[:, 0, cols], sum01[:, :], start=True, stop=False)
                    pe.matmul(turn[0][:, cols], wt1[:, 1, cols], sum2[:, :], start=False, stop=False)
                    step = pe.matmul(turn[0][:, cols], wt1_dense[:, cols], dense[:, bass.ts(bt, P)],
                                     start=False, stop=True)
                step.then_inc(s_top[0], 1)
                pe.wait_ge(s_hid[0], HID1 // P * (bt + 1))
                for m in range(HID2 // P):
                    cols = slice(m * P, (m + 1) * P)
                    for n in range(HID1 // P):
                        step = pe.matmul(turn[1][:, cols], wt2[:, n, cols], hid1[:, n, :], start=n == 0,
                                         stop=n == HID1 // P - 1)
                step.then_inc(s_top[1], 1)
                pe.wait_ge(s_hid[1], HID2 // P * (bt + 1))
                for n in range(HID2 // P):
                    step = pe.matmul(turn[0][0:1, 0:P], wt3[:, n:n + 1], hid2[:, n, :], start=n == 0,
                                     stop=n == HID2 // P - 1)
                step.then_inc(s_top[2], 1)

            def round_(i, q):
                for key in PLAN[q]:
                    if not exists(i, q, key):
                        continue
                    multiply(i, q, key)
                    if key == END[0] and q == 2 and not isinstance(i, int):
                        turn_x(i + 1)
                if q == 4 and not opening(i):
                    dense_layers(i)

            pe.wait_ge(s_ident, 2)
            turn_x(0)
            pe.wait_ge(s_w_ready, 4)
            pe.wait_ge(s_dense_weights, 16 * 7)
            peeled_rounds(pe, round_)


def kernel(**inputs):
    import numpy as np
    import concourse.bacc as bacc
    from concourse.bass_utils import run_bass_kernel_spmd

    a = {name: np.asarray(value) for name, value in inputs.items()}
    nc = bacc.Bacc("TRN2", target_bir_lowering=False, num_devices=1)
    arrays = {}

    def give(name, value):
        name = f"in_{name}"
        arrays[name] = np.ascontiguousarray(value)
        return nc.dram_tensor(name, arrays[name].shape, mybir.dt.from_np(arrays[name].dtype), kind="ExternalInput").ap()

    def pairs(w, swap):
        rows = w.T if not swap else np.concatenate([w.T[:, HALF:], w.T[:, :HALF]], axis=1)
        return rows.reshape(16 // GC, GC, P, P).transpose(0, 2, 1, 3)

    w0 = a["L0_rec_W0"].reshape(P, FIELDS, FIELDS).transpose(1, 2, 0)
    f = np.arange(FIELDS)
    fg = np.stack([w0[f, (f + k) % FIELDS] for k in range(REST)])
    gf = np.stack([w0[(f + k) % FIELDS, f] for k in range(REST)])
    as_chunks = lambda x: x.reshape(SHIFTED, P, P).transpose(1, 0, 2)
    w1, w2 = pairs(a["L0_rec_W1"], True), pairs(a["L0_rec_W2"], False)
    b1 = a["L0_rec_b1"]
    t = {
        "tables": [give(f"tbl_{n}", a[f"tbl_{n}"]) for n in range(FIELDS)],
        "ids": give("ids", a["ids"].reshape(BT, P, FIELDS).transpose(1, 0, 2).reshape(P, BT * FIELDS)),
        "w": {(layer, g): give(f"w{layer}_{g}", as_chunks(fg)[:, GC * g:GC * g + GC] if layer == 0 else (w1, w2)[layer - 1][g])
              for layer, g in KIND},
        "w0_back_first": give("w0_back_first", as_chunks(gf)[FIELDS:, 0]),
        "w0_back": give("w0_back", as_chunks(gf)[:, 1:]),
        "w0_rest": give("w0_rest", w0[f, (f + REST) % FIELDS]),
        "bias": give("bias", np.stack([a["L0_rec_b0"], np.concatenate([b1[HALF:], b1[:HALF]]), a["L0_rec_b2"]], axis=1)),
        "wt1": give("wt1", a["W_top1"][:2 * P].reshape(2, P, HID1).transpose(1, 0, 2)),
        "wt1_dense": give("wt1_dense", a["W_top1"][2 * P:]),
        "wt2": give("wt2", a["W_top2"].reshape(HID1 // P, P, HID2).transpose(1, 0, 2)),
        "wt3": give("wt3", a["W_top3"].reshape(HID2 // P, P).T),
        "bt1": give("bt1", a["b_top1"].reshape(HID1 // P, P).T),
        "bt2": give("bt2", a["b_top2"].reshape(HID2 // P, P).T),
        "dense": give("dense", a["dense_ctx"].T),
    }
    out = nc.dram_tensor("out", (BATCH, 1), F32, kind="ExternalOutput").ap()
    cin_tower(nc, t, out.rearrange("b one -> one b"))
    result = run_bass_kernel_spmd(nc, [arrays], core_ids=[0])
    return result.results[0]["out"]
```

```python
from contextlib import ExitStack

import concourse.bass as bass
from concourse import mybir

F32 = mybir.dt.float32
F32R = mybir.dt.float32r
I32 = mybir.dt.int32
U32 = mybir.dt.uint32
ALU = mybir.AluOpType
ACT = mybir.ActivationFunctionType
AX_X = mybir.AxisListType.X

P = 128
FIELDS, E, BATCH, DENSE = 32, 16, 512, 16
HALF = 64
HID1, HID2 = 512, 256
BT = BATCH // P
EQ = 4
TPB = E // EQ
CT = BT * TPB
N = EQ * P
GC = 2
COPIES = 2
LC = 4
ZSLOTS, SSLOTS = 9, 5
REST = FIELDS // 2
SHIFTED = REST * FIELDS // P

WHOLE, SPLIT = "whole", "split"
WHOLE_AT = (1, 4, 7)
KIND = {(0, g): WHOLE for g in range(SHIFTED // GC)}
KIND |= {(layer, g): WHOLE if g in WHOLE_AT else SPLIT for layer in (1, 2) for g in range(16 // GC)}
SPLITS = [k for k in KIND if KIND[k] == SPLIT]
WHOLES = [k for k in KIND if KIND[k] == WHOLE]

L0, L1, L2 = ([k for k in KIND if k[0] == layer] for layer in range(3))
END = {layer: [k for k in KIND if k[0] == layer][-1] for layer in range(3)}

PLAN = {1: L0 + L1 + L2, 2: L1 + L0 + L2, 3: L1 + L0 + L2, 4: L0 + L2 + L1}
SPLIT_OF = {q: [k for k in PLAN[q] if KIND[k] == SPLIT] for q in PLAN}
DVE_SHARE = {1: (0, 2, 4, 5, 7, 9), 2: (0, 2, 4, 5, 7, 9), 3: (), 4: ()}
BY_DVE = {q: [k for n, k in enumerate(SPLIT_OF[q]) if n in DVE_SHARE[q]] for q in PLAN}
BY_POOL = {q: [k for k in SPLIT_OF[q] if k not in BY_DVE[q]] for q in PLAN}
GATHERS = {1: FIELDS // 2, 2: FIELDS // 2}
GATHERS_AT_ONCE = 4
TURN_AFTER = (2, 6)
DENSE_AFTER = ((1, 2), (1, 4))
DENSE_RELU_AFTER = ((1, 5), (1, 7))
SUM_AFTER = {3: {(1, 5): 0}, 4: {(2, 3): 1, (1, 5): 2}}
TAKE_AFTER = (1, 0)
ROW_AFTER = (2, 3)
RELU_BEHIND = 4
EARLY, LAST = slice(0, BATCH - P), slice(BATCH - P, BATCH)
PER = len(PLAN[1])
assert TPB * PER % ZSLOTS == 0 and TPB * len(SPLITS) % SSLOTS == 0 and all(KIND[k] == WHOLE for k in L0)


def tile(i, q, layer):
    n = q + (1, 0, -1)[layer]
    return i + n // TPB, n % TPB


def opening(i):
    return isinstance(i, int) and i < 0


def exists(i, q, key):
    return not isinstance(i, int) or 0 <= TPB * i + q + (1, 0, -1)[key[0]] < CT


def order(members, i, q):
    return sorted(members[q], key=lambda k: k[0] == 0) if opening(i) and q == 4 else members[q]


def walk(members, i, q, key, step):
    n = order(members, i, q).index(key) + step
    while n < 0:
        i, q = (i - 1, 4) if q == 1 else (i, q - 1)
        n += len(members[q])
    while n >= len(members[q]):
        n -= len(members[q])
        i, q = (i + 1, 1) if q == 4 else (i, q + 1)
    return i, q, order(members, i, q)[n]


def place(members, i, q, key):
    return (i + 1) * sum(map(len, members.values())) + sum(len(members[k]) for k in range(1, q)) + order(members, i, q).index(key)


def first(members):
    return min(place(members, i, q, k) for i in (-1, 0) for q in members for k in order(members, i, q) if exists(i, q, k))


def count(members, i, q, key):
    return place(members, i, q, key) - first(members) + 1


def amount(members, i, q, key):
    n = 1
    while isinstance(i, int) and not exists(*(at := walk(members, i, q, key, n))) and at[0] < BT:
        n += 1
    return n


def user_before(members, ring, i, q, key):
    at = walk(members, i, q, key, -ring)
    while not exists(*at):
        if isinstance(at[0], int) and at[0] < -1:
            return None
        at = walk(members, *at, -ring)
    return at


def groups_back(i, q, key, n):
    at = i, q, key
    while n and not (isinstance(at[0], int) and at[0] < -1):
        at = walk(PLAN, *at, -1)
        n -= exists(*at)
    return at


def zslot(i, q, key):
    return place(PLAN, i if opening(i) else 0, q, key) % ZSLOTS


def sslot(i, q, key):
    return place(SPLIT_OF, i if opening(i) else 0, q, key) % SSLOTS


def peeled_rounds(engine, round_):
    for q in (3, 4):
        round_(-1, q)
    with engine.Fori(0, BT - 1) as i:
        for q in range(1, 5):
            round_(i, q)
    for q in range(1, 5):
        round_(BT - 1, q)


def cin_tower(nc, t, out):
    with ExitStack() as ctx:
        def sb(name, shape, dt=F32):
            return ctx.enter_context(nc.sbuf_tensor(name, shape, dt))

        def bank(name, dt=F32):
            return ctx.enter_context(nc.psum_tensor(name, [P, N], dt))

        def sem(name):
            return ctx.enter_context(nc.semaphore(name))

        xx = nc.dram_tensor("xx", (BT, COPIES * FIELDS, TPB, N), F32).ap()

        ids_all = sb("ids_all", [P, BT * FIELDS], I32)
        ids_now = sb("ids_now", [P, FIELDS], I32)
        emb = sb("emb", [P, FIELDS * E])
        ident = sb("ident", [P, P])
        xt = sb("xt", [P, FIELDS * E // P, P])
        xs = sb("xs", [P, SHIFTED + 2, N])
        xb = sb("xb", [P, 2, FIELDS // 2, N])
        with nc.sbuf_tensor("zl", [P, ZSLOTS, GC, N], F32R) as zl:
            pass
        z = sb("z", [P, ZSLOTS, GC, N])
        zh = sb("zh", [P, SSLOTS, GC, N], F32R)
        zrest = sb("zrest", [P, N], F32R)
        w_whole = sb("w_whole", [P, len(WHOLES), GC, P])
        w_hi = sb("w_hi", [P, len(SPLITS), GC, P], F32R)
        w_lo = sb("w_lo", [P, len(SPLITS), GC, P], F32R)
        w_rest = sb("w_rest", [P, P], F32R)
        keep01 = sb("keep01", [P, TPB * N])
        keep2 = sb("keep2", [P, TPB * N])
        bias = sb("bias", [P, 3])
        wt1 = sb("wt1", [P, 2, HID1])
        wt1_dense = sb("wt1_dense", [DENSE, HID1])
        wt2 = sb("wt2", [P, HID1 // P, HID2])
        wt3 = sb("wt3", [P, HID2 // P])
        bt1 = sb("bt1", [P, HID1 // P])
        bt2 = sb("bt2", [P, HID2 // P])
        dense = sb("dense", [DENSE, BATCH])
        sum01 = sb("sum01", [P, P])
        sum2 = sb("sum2", [P, P])
        hid1 = sb("hid1", [P, HID1 // P, P])
        hid2 = sb("hid2", [P, HID2 // P, BATCH])
        y_row = sb("y_row", [1, BATCH])

        y = [bank(f"y{l}") for l in range(3)]
        h1 = bank("h1")
        h2 = [bank("h2a"), bank("h2b")]
        top = [bank("top0"), bank("top1")]

        stage_all = z[:, :, :, :].rearrange("p s c n -> p (s c n)").rearrange("p (k n) -> p k n", n=P)
        stage = stage_all[:, 0:GC * len(SPLITS), :].rearrange("p (k c) n -> p k c n", c=GC)
        stage_back = stage_all[:, GC * len(SPLITS):GC * len(SPLITS) + SHIFTED, :]
        stage_rest = stage_all[:, GC * len(SPLITS) + SHIFTED, :]

        s_ids = sem("s_ids")
        s_zero = sem("s_zero")
        s_weights = sem("s_weights")
        s_dense_weights = sem("s_dense_weights")
        s_ident = sem("s_ident")
        s_w_rounded = sem("s_w_rounded")
        s_w_ready = sem("s_w_ready")
        s_emb = sem("s_emb")
        s_turned = sem("s_turned")
        s_xt = sem("s_xt")
        s_xx = sem("s_xx")
        s_xs = sem("s_xs")
        s_xb = [[sem(f"s_xb{k}_{g}") for g in range(16 // LC)] for k in range(2)]
        s_z_ready = sem("s_z_ready")
        s_z_used = sem("s_z_used")
        s_zh = sem("s_zh")
        s_zl_pool = sem("s_zl_pool")
        s_zl_dve = sem("s_zl_dve")
        s_rest = sem("s_rest")
        s_rest_hi = sem("s_rest_hi")
        s_rest_ready = sem("s_rest_ready")
        s_y0 = sem("s_y0")
        s_relu = [sem(f"s_relu{l}") for l in range(3)]
        s_sum = [sem(f"s_sum{l}") for l in range(3)]
        s_top = [sem(f"s_top{l}") for l in range(3)]
        s_hid = [sem(f"s_hid{l}") for l in range(2)]
        s_row = sem("s_row")
        s_out = sem("s_out")

        block = ctx.enter_context(nc.Block())

        def number(i, q):
            return TPB * i + q

        def relus(layer, tiles):
            return tiles + 1 if layer == 2 else 3 * tiles

        @block.sync
        def _(sp):
            def store_x(bt):
                sp.wait_ge(s_xt, bt + 1)
                for c in range(COPIES):
                    rows = xx[bt, c * FIELDS:(c + 1) * FIELDS, :, :].rearrange(
                        "(g f) k (e b) -> (f k e) g b", g=FIELDS * E // P, b=P)
                    sp.dma_start(rows, xt[:, :, :]).then_inc(s_xx, 16)
                sp.wait_ge(s_xx, 16 * COPIES * (bt + 1))

            def load_shifted(bt, k):
                for n, row in enumerate((0, REST)):
                    sp.dma_start(xs[:, SHIFTED + n, :], rows_from(bt, row, k, [0, 4], [1, FIELDS])).then_inc(s_xs, 16)
                for r in range(4):
                    sp.dma_start(xs[r * FIELDS:(r + 1) * FIELDS, 0:SHIFTED, :],
                                 rows_from(bt, r, k, [1, FIELDS], [4, SHIFTED])).then_inc(s_xs, 16)

            def rows_from(bt, row, k, *dims):
                start = xx[bt, row:row + 1, k, :]
                return bass.AP(start.tensor, start.offset, [[step * TPB * N, n] for step, n in dims] + [[1, N]])

            def load_broadcast(bt, k, g):
                pairs = xx[bt, 0:FIELDS, k, :].rearrange("(j two) n -> two j n", two=2)
                for half in range(2):
                    sp.dma_start(xb[half * HALF:(half + 1) * HALF, k % 2, LC * g:LC * g + LC, :],
                                 pairs[half, LC * g:LC * g + LC, :].partition_broadcast(HALF)
                                 ).then_inc(s_xb[k % 2][g], 16)

            sp.dma_start(ids_all[:, :], t["ids"]).then_inc(s_ids, 16)
            for n, key in enumerate(SPLITS):
                sp.dma_start(stage[:, n, :, :], t["w"][key]).then_inc(s_weights, 16)
            for n, key in enumerate(WHOLES):
                sp.dma_start(w_whole[:, n, :, :], t["w"][key]).then_inc(s_weights, 16)
            sp.dma_start(stage_back[FIELDS:P, 0, :], t["w0_back_first"]).then_inc(s_weights, 16)
            sp.dma_start(stage_back[:, 1:SHIFTED, :], t["w0_back"]).then_inc(s_weights, 16)
            for r in range(4):
                sp.dma_start(stage_rest[r * FIELDS:(r + 1) * FIELDS, :], t["w0_rest"]).then_inc(s_weights, 16)
            sp.dma_start(bias[:, :], t["bias"]).then_inc(s_weights, 16)
            for dst, src in ((wt1[:, :, :], t["wt1"]), (wt1_dense[:, :], t["wt1_dense"]), (wt2[:, :, :], t["wt2"]),
                             (wt3[:, :], t["wt3"]), (bt1[:, :], t["bt1"]), (bt2[:, :], t["bt2"]),
                             (dense[:, :], t["dense"])):
                sp.dma_start(dst, src).then_inc(s_dense_weights, 16)

            def round_(i, q):
                r = number(i, q)

                def shifted():
                    if exists(i, q + 1, (0, 0)):
                        if q != 2:
                            sp.wait_ge(s_rest_ready, r + 2)
                        load_shifted(i + (q + 2) // TPB, (q + 2) % TPB)

                if q != 2 and not (opening(i) and q == 4):
                    shifted()
                if exists(i, q, (0, 0)) and exists(i, q, (1, 0)):
                    for g in range(16 // LC):
                        if exists(i, q, (2, 0)):
                            sp.wait_ge(s_z_ready, count(PLAN, i, q, (2, LC // GC * (g + 1) - 1)))
                        load_broadcast(*tile(i, q, 0), g)
                        if opening(i) and g == 1:
                            shifted()
                if q == 2:
                    if exists(i + 1, 1, (1, 0)):
                        store_x(i + 1)
                    shifted()

            store_x(0)
            load_shifted(0, 0)
            for g in range(16 // LC):
                load_broadcast(0, 0, g)
            peeled_rounds(sp, round_)
            sp.wait_ge(s_row, 2)
            sp.dma_start(out, y_row[:, :]).then_inc(s_out, 16)
            sp.wait_ge(s_out, 16)

        @block.gpsimd
        def _(pool):
            def take_ids(bt):
                if not isinstance(bt, int):
                    pool.wait_ge(s_turned, bt)
                pool.tensor_copy(ids_now[:, :], ids_all[:, bass.ts(bt, FIELDS)])
                pool.drain()

            def gather(f):
                pool.indirect_dma_start(
                    emb[:, f * E:(f + 1) * E], None, t["tables"][f],
                    bass.IndirectOffsetOnAxis(ap=ids_now[:, f:f + 1].bitcast(U32), axis=0)).then_inc(s_emb, 16)

            def round_(i, q):
                gathers = []
                if q in GATHERS and not isinstance(i, int):
                    before = sum(GATHERS[k] for k in range(1, q))
                    gathers = list(range(before, before + GATHERS[q]))
                    if q == 1:
                        take_ids(i + 1)
                for key in order(BY_POOL, i, q):
                    for f in gathers[:GATHERS_AT_ONCE]:
                        gather(gathers.pop(0))
                    if not exists(i, q, key):
                        continue
                    pool.wait_ge(s_zh, count(SPLIT_OF, i, q, key))
                    slot = zslot(i, q, key)
                    pool.tensor_tensor(zl[:, slot, :, :], z[:, slot, :, :], zh[:, sslot(i, q, key), :, :].bitcast(F32),
                                       ALU.subtract).then_inc(s_zl_pool, amount(BY_POOL, i, q, key))
                for f in gathers:
                    gather(f)

            pool.memset(ident[:, :], 0.0).then_inc(s_ident, 1)
            pool.wait_ge(s_ids, 16)
            take_ids(0)
            for f in range(FIELDS):
                gather(f)
            pool.wait_ge(s_ident, 1)
            pool.affine_select(out=ident[:, :], in_=ident[:, :], compare_op=ALU.not_equal, fill=1.0, base=0,
                               pattern=[[-1, P]], channel_multiplier=1).then_inc(s_ident, 1)
            peeled_rounds(pool, round_)

        @block.scalar
        def _(act):
            def take_x(bt):
                if not isinstance(bt, int):
                    act.wait_ge(s_xx, 16 * COPIES * bt)
                act.wait_ge(s_turned, bt + 1)
                act.activation(xt[:, :, :], top[1][:, :].rearrange("p (g b) -> p g b", b=P), ACT.Copy).then_inc(s_xt, 1)

            def round_z(i, q, key):
                act.wait_ge(s_z_ready, count(PLAN, i, q, key))
                if user := user_before(SPLIT_OF, SSLOTS, i, q, key):
                    act.wait_ge(s_z_used, count(PLAN, *user))
                act.activation(zh[:, sslot(i, q, key), :, :], z[:, zslot(i, q, key), :, :],
                               ACT.Copy).then_inc(s_zh, amount(SPLIT_OF, i, q, key))

            def round_rest(c):
                act.wait_ge(s_rest, c + 1)
                if not (isinstance(c, int) and c == 0):
                    act.wait_ge(s_y0, c)
                act.activation(zrest[:, :], xs[:, SHIFTED + 1, :], ACT.Copy).then_inc(s_rest_hi, 1)

            def relu(layer, i, q):
                bt, k = tile(i, q, layer)
                c = TPB * bt + k
                if layer == 0:
                    act.wait_ge(s_y0, c + 1)
                else:
                    act.wait_ge(s_z_used, count(PLAN, i, q, END[layer]))
                if k == 0:
                    act.wait_ge(s_sum[layer], bt + 1)
                cols = slice(k * N, (k + 1) * N)
                if layer == 2:
                    act.activation(keep2[:, cols], y[2][:, :], ACT.Relu, bias=bias[:, 2:3]).then_inc(s_relu[2], 1)
                    return
                kept, passed = (slice(0, HALF), slice(HALF, P)) if layer == 0 else (slice(HALF, P), slice(0, HALF))
                if layer == 0 and exists(i, q, END[1]):
                    act.wait_ge(s_z_ready, count(PLAN, i, q, END[1]))
                if layer == 1 and (at := walk(PLAN, i, q, END[1], -PER)) and exists(*at[:2], END[2]):
                    act.wait_ge(s_z_ready, count(PLAN, *at[:2], END[2]))
                h = h1 if layer == 0 else h2[k % 2]
                for half in (slice(0, HALF), slice(HALF, P)):
                    act.activation(h[half, :], y[layer][passed, :], ACT.Relu,
                                   bias=bias[passed, layer:layer + 1]).then_inc(s_relu[layer], 1)
                act.activation(keep01[kept, cols], y[layer][kept, :], ACT.Relu,
                               bias=bias[kept, layer:layer + 1]).then_inc(s_relu[layer], 1)

            def relu0_after_layer1(i, q):
                return q in (1, 4) and not opening(i)

            def dense_relu(bt, layer):
                act.wait_ge(s_top[layer], bt + (2 if layer == 0 else 1))
                width, b = ((HID1, bt1), (HID2, bt2))[layer]
                for m in range(width // P):
                    hid = hid1[:, m, :] if layer == 0 else hid2[:, m, bass.ts(bt, P)]
                    act.activation(hid, top[layer][:, m * P:(m + 1) * P], ACT.Relu,
                                   bias=b[:, m:m + 1]).then_inc(s_hid[layer], 1)

            def take_row(n, cols):
                act.wait_ge(s_top[2], n)
                act.activation(y_row[:, cols], top[0][0:1, 0:cols.stop - cols.start], ACT.Copy).then_inc(s_row, 1)

            def round_(i, q):
                dense = [0, 1] if q == 4 and not opening(i) else []
                for key in order(PLAN, i, q):
                    if not exists(i, q, key):
                        continue
                    if key == END[0]:
                        round_rest(number(i, q) + 1)
                    if KIND[key] == SPLIT:
                        round_z(i, q, key)
                    *at, ended = groups_back(i, q, key, RELU_BEHIND)
                    if (ended == END[ended[0]] and not opening(i)
                            and not (ended == END[0] and relu0_after_layer1(*at))):
                        relu(ended[0], *at)
                    if key == END[1] and exists(i, q, END[0]) and relu0_after_layer1(i, q):
                        relu(0, i, q)
                    if q == 3 and not isinstance(i, int) and key == TAKE_AFTER:
                        take_x(i + 1)
                    if q == 1 and isinstance(i, int) and key == ROW_AFTER:
                        take_row(1, EARLY)
                    if dense and key == DENSE_RELU_AFTER[dense[0]]:
                        dense_relu(i, dense.pop(0))
                if opening(i):
                    relu(0, i, q)
                if isinstance(i, int) and q == 4 and not opening(i):
                    relu(2, i, q)
                    for layer in dense:
                        dense_relu(i, layer)
                    take_row(2, LAST)

            act.wait_ge(s_weights, 16 * (len(KIND) + 7))
            act.activation(w_hi[:, :, :, :], stage[:, 0:len(SPLITS), :, :], ACT.Copy).then_inc(s_w_rounded, 1)
            act.activation(w_rest[:, :], stage_rest, ACT.Copy).then_inc(s_w_rounded, 1)
            act.wait_ge(s_dense_weights, 16 * 7)
            take_x(0)
            peeled_rounds(act, round_)

        @block.vector
        def _(dve):
            def make_z(i, q, key):
                layer, g = key
                bt, k = tile(i, q, layer)
                c = TPB * bt + k
                if user := user_before(PLAN, ZSLOTS, i, q, key):
                    dve.wait_ge(s_z_used, count(PLAN, *user))
                dst = z[:, zslot(i, q, key), :, :]
                if layer == 0:
                    dve.wait_ge(s_xs, 16 * 6 * (c + 1))
                    x = xs[:, SHIFTED, :]
                    dve.tensor_tensor(dst, xs[:, GC * g:GC * g + GC, :], x.unsqueeze(1).broadcast_to([P, GC, N]),
                                      ALU.mult).then_inc(s_z_ready, amount(PLAN, i, q, key))
                    if key == END[0]:
                        dve.tensor_tensor(xs[:, SHIFTED + 1, :], xs[:, SHIFTED + 1, :], x, ALU.mult).then_inc(s_rest, 1)
                    return
                dve.wait_ge(s_relu[layer - 1], 3 * c + 2)
                if layer == 1:
                    dve.wait_ge(s_xb[k % 2][GC * g // LC], 32 * (TPB // 2 * bt + k // 2 + 1))
                h = h1 if layer == 1 else h2[k % 2]
                dve.tensor_tensor(dst, xb[:, k % 2, GC * g:GC * g + GC, :], h[:, :].unsqueeze(1).broadcast_to([P, GC, N]),
                                  ALU.mult).then_inc(s_z_ready, amount(PLAN, i, q, key))

            def make_zl(i, q, key):
                dve.wait_ge(s_zh, count(SPLIT_OF, i, q, key))
                slot = zslot(i, q, key)
                dve.tensor_tensor(zl[:, slot, :, :], z[:, slot, :, :], zh[:, sslot(i, q, key), :, :].bitcast(F32),
                                  ALU.subtract).then_inc(s_zl_dve, amount(BY_DVE, i, q, key))

            def make_rest(c):
                dve.wait_ge(s_rest_hi, c + 1)
                dve.tensor_tensor(zrest[HALF:P, :], xs[HALF:P, SHIFTED + 1, :], zrest[HALF:P, :].bitcast(F32),
                                  ALU.subtract).then_inc(s_rest_ready, 1)

            def sum_kept(layer, bt):
                kept, dst, rows = ((keep01, sum01, slice(0, HALF)), (keep01, sum01, slice(HALF, P)),
                                   (keep2, sum2, slice(0, P)))[layer]
                dve.wait_ge(s_relu[layer], relus(layer, TPB * (bt + 1)))
                dve.wait_ge(s_top[0], bt + 1)
                dve.tensor_reduce(dst[rows, :], kept[rows, :].rearrange("p (e b) -> p b e", b=P), AX_X,
                                  ALU.add).then_inc(s_sum[layer], 1)

            def subtract(i, q, key):
                if key in BY_DVE[q]:
                    make_zl(i, q, key)
                if key == END[0]:
                    make_rest(number(i, q) + 1)

            def round_(i, q):
                behind = None
                for key in order(PLAN, i, q):
                    if not exists(i, q, key):
                        continue
                    make_z(i, q, key)
                    if behind:
                        subtract(i, q, behind)
                    behind = key
                    if not opening(i) and key in SUM_AFTER.get(q, ()):
                        sum_kept(SUM_AFTER[q][key], i)
                subtract(i, q, behind)
                if q == 4 and not opening(i) and not exists(i, q, END[1]):
                    sum_kept(2, i)

            for n, counter in enumerate((*s_sum, s_relu[2], s_top[0], s_hid[1])):
                dve.memset(keep01[:, n:n + 1], 0.0).then_inc(counter, 1)
            dve.memset(stage_back[0:FIELDS, 0, :], 0.0).then_inc(s_zero, 1)
            dve.wait_ge(s_zero, 1)
            dve.wait_ge(s_weights, 16 * (len(KIND) + 7))
            folded = w_whole[:, 0:len(L0), :, :].rearrange("p g c n -> p (g c) n")
            dve.tensor_tensor(folded, folded, stage_back, ALU.add).then_inc(s_w_ready, 1)
            dve.wait_ge(s_w_rounded, 2)
            dve.tensor_tensor(w_lo[:, :, :, :], stage[:, 0:len(SPLITS), :, :], w_hi[:, :, :, :].bitcast(F32),
                              ALU.subtract).then_inc(s_w_ready, 1)
            for r in (1, 3):
                rows = slice(r * FIELDS, (r + 1) * FIELDS)
                dve.tensor_tensor(w_rest[rows, :], stage_rest[rows, :], w_rest[rows, :].bitcast(F32),
                                  ALU.subtract).then_inc(s_w_ready, 1)
            dve.wait_ge(s_w_ready, 4)
            peeled_rounds(dve, round_)

        @block.tensor
        def _(pe):
            def turn_x(bt):
                pe.wait_ge(s_emb, 16 * FIELDS * (bt + 1))
                if not isinstance(bt, int):
                    pe.wait_ge(s_hid[1], HID2 // P * (bt - 1) + 1)
                for g in range(FIELDS * E // P):
                    cols = slice(g * P, (g + 1) * P)
                    step = pe.transpose(top[1][:, cols], emb[:, cols], ident[:, :])
                step.then_inc(s_turned, 1)

            def multiply_lower(i, q, key):
                if key in BY_POOL[q]:
                    pe.wait_ge(s_zl_pool, count(BY_POOL, i, q, key))
                else:
                    pe.wait_ge(s_zl_dve, count(BY_DVE, i, q, key))
                for j in range(GC):
                    step = pe.matmul(y[key[0]][:, :], w_hi[:, SPLITS.index(key), j, :], zl[:, zslot(i, q, key), j, :],
                                     start=False, stop=key == END[key[0]] and j == GC - 1)
                step.then_inc(s_z_used, amount(PLAN, i, q, key))

            def multiply(i, q, key, behind):
                layer, g = key
                bt, k = tile(i, q, layer)
                c = TPB * bt + k
                acc = y[layer][:, :]
                if g == 0 and not (isinstance(c, int) and c == 0):
                    pe.wait_ge(s_relu[layer], relus(layer, c))
                if KIND[key] == WHOLE:
                    w, zs = w_whole[:, WHOLES.index(key), :, :], z[:, zslot(i, q, key), :, :]
                    pe.wait_ge(s_z_ready, count(PLAN, i, q, key))
                    for j in range(GC):
                        if j == GC - 1 and behind:
                            multiply_lower(i, q, behind)
                        step = pe.matmul(acc, w[:, j, :], zs[:, j, :], start=g == 0 and j == 0,
                                         stop=layer > 0 and key == END[layer] and j == GC - 1)
                    step.then_inc(s_z_used, amount(PLAN, i, q, key))
                else:
                    n, s = SPLITS.index(key), sslot(i, q, key)
                    pe.wait_ge(s_zh, count(SPLIT_OF, i, q, key))
                    for j in range(GC):
                        pe.matmul(acc, w_hi[:, n, j, :], zh[:, s, j, :], start=g == 0 and j == 0, stop=False)
                        pe.matmul(acc, w_lo[:, n, j, :], zh[:, s, j, :], start=False, stop=False)
                    if behind:
                        multiply_lower(i, q, behind)
                    if key == END[layer]:
                        multiply_lower(i, q, key)
                if key == END[0]:
                    pe.wait_ge(s_rest_ready, c + 1)
                    pe.matmul(acc, w_rest[:, :], zrest[:, :], start=False, stop=True).then_inc(s_y0, 1)

            def dense_products(bt, layer):
                if layer == 0:
                    for n in range(3):
                        pe.wait_ge(s_sum[n], bt + 2)
                    if isinstance(bt, int):
                        pe.wait_ge(s_row, 1)
                    else:
                        pe.wait_ge(s_xt, bt + 2)
                    for m in range(HID1 // P):
                        cols = slice(m * P, (m + 1) * P)
                        pe.matmul(top[0][:, cols], wt1[:, 0, cols], sum01[:, :], start=True, stop=False)
                        pe.matmul(top[0][:, cols], wt1[:, 1, cols], sum2[:, :], start=False, stop=False)
                        step = pe.matmul(top[0][:, cols], wt1_dense[:, cols], dense[:, bass.ts(bt, P)],
                                         start=False, stop=True)
                elif layer == 1:
                    pe.wait_ge(s_hid[0], HID1 // P * (bt + 1))
                    for m in range(HID2 // P):
                        cols = slice(m * P, (m + 1) * P)
                        for n in range(HID1 // P):
                            step = pe.matmul(top[1][:, cols], wt2[:, n, cols], hid1[:, n, :], start=n == 0,
                                             stop=n == HID1 // P - 1)
                step.then_inc(s_top[layer], 1)

            def output_row(cols):
                pe.wait_ge(s_hid[1], HID2 // P * (cols.stop // P) + 1)
                for n in range(HID2 // P):
                    step = pe.matmul(top[0][0:1, 0:cols.stop - cols.start], wt3[:, n:n + 1], hid2[:, n, cols],
                                     start=n == 0, stop=n == HID2 // P - 1)
                step.then_inc(s_top[2], 1)

            def round_(i, q):
                layers = [0, 1] if q == 4 and not opening(i) else []
                behind = None
                for key in order(PLAN, i, q):
                    if not exists(i, q, key):
                        continue
                    multiply(i, q, key, behind)
                    behind = key if KIND[key] == SPLIT and key != END[key[0]] else None
                    if q == 2 and not isinstance(i, int) and key == TURN_AFTER:
                        turn_x(i + 1)
                    if layers and key == DENSE_AFTER[layers[0]]:
                        dense_products(i, layers.pop(0))
                    if isinstance(i, int) and q == 1 and key == END[1]:
                        output_row(EARLY)
                for layer in layers:
                    dense_products(i, layer)
                if isinstance(i, int) and q == 4 and not opening(i):
                    output_row(LAST)

            pe.wait_ge(s_ident, 2)
            turn_x(0)
            pe.wait_ge(s_w_ready, 4)
            pe.wait_ge(s_dense_weights, 16 * 7)
            peeled_rounds(pe, round_)


def kernel(**inputs):
    import numpy as np
    import concourse.bacc as bacc
    from concourse.bass_utils import run_bass_kernel_spmd

    a = {name: np.asarray(value) for name, value in inputs.items()}
    nc = bacc.Bacc("TRN2", target_bir_lowering=False, num_devices=1)
    arrays = {}

    def give(name, value):
        name = f"in_{name}"
        arrays[name] = np.ascontiguousarray(value)
        return nc.dram_tensor(name, arrays[name].shape, mybir.dt.from_np(arrays[name].dtype), kind="ExternalInput").ap()

    def pairs(w, swap):
        rows = w.T if not swap else np.concatenate([w.T[:, HALF:], w.T[:, :HALF]], axis=1)
        return rows.reshape(16 // GC, GC, P, P).transpose(0, 2, 1, 3)

    w0 = a["L0_rec_W0"].reshape(P, FIELDS, FIELDS).transpose(1, 2, 0)
    f = np.arange(FIELDS)
    fg = np.stack([w0[f, (f + k) % FIELDS] for k in range(REST)])
    gf = np.stack([w0[(f + k) % FIELDS, f] for k in range(REST)])
    as_chunks = lambda x: x.reshape(SHIFTED, P, P).transpose(1, 0, 2)
    w1, w2 = pairs(a["L0_rec_W1"], True), pairs(a["L0_rec_W2"], False)
    b1 = a["L0_rec_b1"]
    t = {
        "tables": [give(f"tbl_{n}", a[f"tbl_{n}"]) for n in range(FIELDS)],
        "ids": give("ids", a["ids"].reshape(BT, P, FIELDS).transpose(1, 0, 2).reshape(P, BT * FIELDS)),
        "w": {(layer, g): give(f"w{layer}_{g}",
                               as_chunks(fg)[:, GC * g:GC * g + GC] if layer == 0 else (w1, w2)[layer - 1][g])
              for layer, g in KIND},
        "w0_back_first": give("w0_back_first", as_chunks(gf)[FIELDS:, 0]),
        "w0_back": give("w0_back", as_chunks(gf)[:, 1:]),
        "w0_rest": give("w0_rest", w0[f, (f + REST) % FIELDS]),
        "bias": give("bias", np.stack([a["L0_rec_b0"], np.concatenate([b1[HALF:], b1[:HALF]]), a["L0_rec_b2"]], axis=1)),
        "wt1": give("wt1", a["W_top1"][:2 * P].reshape(2, P, HID1).transpose(1, 0, 2)),
        "wt1_dense": give("wt1_dense", a["W_top1"][2 * P:]),
        "wt2": give("wt2", a["W_top2"].reshape(HID1 // P, P, HID2).transpose(1, 0, 2)),
        "wt3": give("wt3", a["W_top3"].reshape(HID2 // P, P).T),
        "bt1": give("bt1", a["b_top1"].reshape(HID1 // P, P).T),
        "bt2": give("bt2", a["b_top2"].reshape(HID2 // P, P).T),
        "dense": give("dense", a["dense_ctx"].T),
    }
    out = nc.dram_tensor("out", (BATCH, 1), F32, kind="ExternalOutput").ap()
    cin_tower(nc, t, out.rearrange("b one -> one b"))
    result = run_bass_kernel_spmd(nc, [arrays], core_ids=[0])
    return result.results[0]["out"]
```
